# Optimizing a Trainium2 kernel written in Bass

```python
import numpy as np
import jax
import jax.numpy as jnp

def _softmax(x, axis=-1):
    return jax.nn.softmax(x, axis=axis)

def _gelu(x):
    return jax.nn.gelu(x, approximate=True)

def _silu(x):
    return jax.nn.silu(x)

def _sigmoid(x):
    return jax.nn.sigmoid(x)

def _layernorm(x, axis=-1, eps=1e-05):
    m = jnp.mean(x, axis=axis, keepdims=True)
    v = jnp.var(x, axis=axis, keepdims=True)
    return (x - m) / jnp.sqrt(v + eps)

def _scatter_add(tgt, idx, src, axis=0):
    return tgt.at[idx].add(src)

def _segment_sum(src, seg, n):
    return jax.ops.segment_sum(src, seg, n)
kernel_name = 'mk_decoder_preln_d1_seqx_r8_3a4801'

def setup_inputs(seed: int=0):
    np.random.seed(seed)
    _w = jnp.asarray

    def _rec_inputs():
        import jax
        import jax.numpy as jnp
        _rk = jax.random.key(seed)
        x = -0.0002928 + 1 * jax.random.normal(jax.random.fold_in(_rk, 1), (32, 128, 128), jnp.float32)
        _lenS = 128 - jax.random.randint(jax.random.fold_in(_rk, 7), (32,), 0, max(1, 128 // 4) + 1, jnp.int32)
        _lenS2 = 128 - jax.random.randint(jax.random.fold_in(_rk, 8), (32,), 0, max(1, 128 // 4) + 1, jnp.int32)
        _ctx_1024P = jax.random.normal(jax.random.fold_in(_rk, 11), (32, 16, 128), jnp.float32)
        _ctx_1024c = jax.random.dirichlet(jax.random.fold_in(_rk, 511), 0.3 * jnp.ones((16,), jnp.float32), (32, 128))
        _ctx_1024t = jnp.einsum('bsk,bkd->bsd', _ctx_1024c, _ctx_1024P)
        _ctx_1024t = _ctx_1024t * jax.lax.rsqrt(jnp.mean(jnp.square(_ctx_1024t)) + 1e-12) * 0.953939
        ctx_1024 = -1.39393e-06 + 0.999914 * (_ctx_1024t + 0.3 * jax.random.normal(jax.random.fold_in(_rk, 611), (32, 128, 128), jnp.float32))
        _validS = jnp.arange(128)[None, :] < _lenS[:, None]
        _validS2 = jnp.arange(128)[None, :] < _lenS2[:, None]
        _causal = jnp.tril(jnp.ones((128, 128), dtype=bool))
        mask_Bx1xS2_ik0 = jnp.where(jnp.broadcast_to(_validS2[:, None, :], (32, 1, 128)), 0, 1).astype(jnp.int32)
        return (x, ctx_1024, mask_Bx1xS2_ik0)
    x, ctx_1024, mask_Bx1xS2_ik0 = _rec_inputs()

    def _L0_attn_setup():
        import jax, jax.numpy as jnp
        import numpy as np
        D_OUT = 128
        key = jax.random.key(seed)
        k1, k2 = jax.random.split(key)
        x = jax.random.normal(k1, (4, 256, 128), dtype=jnp.float32)
        W_qkv = jax.random.normal(k2, (128, 3 * D_OUT), dtype=jnp.float32) * 0.02
        return {'x': x, 'W_qkv': W_qkv}
    _L0_attn_all = _L0_attn_setup()
    _L0_attn_in = {k: v for k, v in _L0_attn_all.items() if k in ('W_qkv',)}
    del _L0_attn_all

    def _L0_xattn_setup():
        import jax, jax.numpy as jnp
        import numpy as np
        H = 16
        D_MODEL = 128
        D_K = D_MODEL // H
        NEG = -1000000000.0

        def _split_heads(x, B, S):
            return x.reshape(B, S, H, D_K).transpose(0, 2, 1, 3)
        key = jax.random.key(seed)
        ks = jax.random.split(key, 13)
        B, S = (2, 256)
        std = 1.0 / np.sqrt(D_MODEL)
        inp = {'query': jax.random.normal(ks[0], (B, S, D_MODEL), jnp.float32), 'key': jax.random.normal(ks[1], (B, S, D_MODEL), jnp.float32), 'value': jax.random.normal(ks[2], (B, S, D_MODEL), jnp.float32), 'mask': jax.random.randint(ks[3], (B, 1, S), 0, 2, jnp.int32), 'Wq': jax.random.normal(ks[4], (D_MODEL, D_MODEL), jnp.float32) * std, 'bq': jax.random.normal(ks[5], (D_MODEL,), jnp.float32) * std, 'Wk': jax.random.normal(ks[6], (D_MODEL, D_MODEL), jnp.float32) * std, 'bk': jax.random.normal(ks[7], (D_MODEL,), jnp.float32) * std, 'Wv': jax.random.normal(ks[8], (D_MODEL, D_MODEL), jnp.float32) * std, 'bv': jax.random.normal(ks[9], (D_MODEL,), jnp.float32) * std, 'Wo': jax.random.normal(ks[10], (D_MODEL, D_MODEL), jnp.float32) * std, 'bo': jax.random.normal(ks[11], (D_MODEL,), jnp.float32) * std}
        return inp
    _L0_xattn_all = _L0_xattn_setup()
    _L0_xattn_in = {k: v for k, v in _L0_xattn_all.items() if k in ('Wq', 'bq', 'Wk', 'bk', 'Wv', 'bv', 'Wo', 'bo')}
    del _L0_xattn_all

    def _L0_ffn_setup():
        import jax, jax.numpy as jnp
        import numpy as np
        BLOCK = 32
        W_BITS = 4
        ACT_BITS = 16

        def act_qdq(x):
            qmax = 2.0 ** (ACT_BITS - 1) - 1.0
            scale = jnp.maximum(jnp.max(jnp.abs(x)) / qmax, 1e-12)
            return jnp.clip(jnp.round(x / scale), -qmax - 1.0, qmax) * scale

        def fixed_qdq_u16(x):
            scale = 1.0 / 65536.0
            return jnp.clip(jnp.round(x / scale), 0.0, 65535.0) * scale

        def lpbq_dequant(w):
            O, I = w.shape
            qmax = 2.0 ** (W_BITS - 1) - 1.0
            wb = w.reshape(O, I // BLOCK, BLOCK)
            s = jnp.maximum(jnp.max(jnp.abs(wb), axis=-1, keepdims=True) / qmax, 1e-12)
            wq = jnp.clip(jnp.round(wb / s), -qmax - 1.0, qmax) * s
            return wq.reshape(O, I)
        key = jax.random.key(seed)
        k1, k2, k3, k4 = jax.random.split(key, 4)
        B, S, H, I = (2, 512, 128, 384)
        x = jax.random.normal(k1, (B, S, H), jnp.float32)
        w_gate = jax.random.normal(k2, (I, H), jnp.float32) * 0.02
        w_up = jax.random.normal(k3, (I, H), jnp.float32) * 0.02
        w_down = jax.random.normal(k4, (H, I), jnp.float32) * 0.02
        return {'x': x, 'w_gate': w_gate, 'w_up': w_up, 'w_down': w_down}
    _L0_ffn_all = _L0_ffn_setup()
    _L0_ffn_in = {k: v for k, v in _L0_ffn_all.items() if k in ('w_gate', 'w_up', 'w_down')}
    del _L0_ffn_all
    return {'x': x, 'ctx_1024': ctx_1024, 'mask_Bx1xS2_ik0': mask_Bx1xS2_ik0, 'L0_attn_W_qkv': _L0_attn_in['W_qkv'], 'L0_xattn_Wq': _L0_xattn_in['Wq'], 'L0_xattn_bq': _L0_xattn_in['bq'], 'L0_xattn_Wk': _L0_xattn_in['Wk'], 'L0_xattn_bk': _L0_xattn_in['bk'], 'L0_xattn_Wv': _L0_xattn_in['Wv'], 'L0_xattn_bv': _L0_xattn_in['bv'], 'L0_xattn_Wo': _L0_xattn_in['Wo'], 'L0_xattn_bo': _L0_xattn_in['bo'], 'L0_ffn_w_gate': _L0_ffn_in['w_gate'], 'L0_ffn_w_up': _L0_ffn_in['w_up'], 'L0_ffn_w_down': _L0_ffn_in['w_down']}

def reference(x, ctx_1024, mask_Bx1xS2_ik0, L0_attn_W_qkv, L0_xattn_Wq, L0_xattn_bq, L0_xattn_Wk, L0_xattn_bk, L0_xattn_Wv, L0_xattn_bv, L0_xattn_Wo, L0_xattn_bo, L0_ffn_w_gate, L0_ffn_w_up, L0_ffn_w_down):
    import jax
    import jax.numpy as jnp

    def _L0_attn_ref(x, W_qkv):
        import jax, jax.numpy as jnp
        import numpy as np
        D_OUT = 128
        B, N, _ = x.shape
        scale = D_OUT ** 0.5
        qkv = jnp.einsum('bnd,de->bne', x, W_qkv)
        q, k, v = jnp.split(qkv, 3, axis=-1)
        scores = jnp.einsum('bnd,bmd->bnm', q, k) / scale
        causal = jnp.triu(jnp.ones((N, N), dtype=bool), k=1)
        scores = jnp.where(causal, -jnp.inf, scores)
        attn = jax.nn.softmax(scores, axis=-1)
        return jnp.einsum('bnm,bmd->bnd', attn, v)

    def _L0_xattn_ref(query, key, value, mask, Wq, bq, Wk, bk, Wv, bv, Wo, bo):
        import jax, jax.numpy as jnp
        import numpy as np
        H = 16
        D_MODEL = 128
        D_K = D_MODEL // H
        NEG = -1000000000.0

        def _split_heads(x, B, S):
            return x.reshape(B, S, H, D_K).transpose(0, 2, 1, 3)
        B, S, _ = query.shape
        q = _split_heads(query @ Wq.T + bq, B, S)
        k = _split_heads(key @ Wk.T + bk, B, S)
        v = _split_heads(value @ Wv.T + bv, B, S)
        scores = jnp.einsum('bhqd,bhkd->bhqk', q, k) / jnp.sqrt(jnp.float32(D_K))
        m = mask[:, None, :, :]
        scores = jnp.where(m == 0, jnp.float32(NEG), scores)
        p_attn = jax.nn.softmax(scores, axis=-1)
        x = jnp.einsum('bhqk,bhkd->bhqd', p_attn, v)
        x = x.transpose(0, 2, 1, 3).reshape(B, S, H * D_K)
        return x @ Wo.T + bo

    def _L0_ffn_ref(x, w_gate, w_up, w_down):
        import jax, jax.numpy as jnp
        import numpy as np
        BLOCK = 32
        W_BITS = 4
        ACT_BITS = 16

        def act_qdq(x):
            qmax = 2.0 ** (ACT_BITS - 1) - 1.0
            scale = jnp.maximum(jnp.max(jnp.abs(x)) / qmax, 1e-12)
            return jnp.clip(jnp.round(x / scale), -qmax - 1.0, qmax) * scale

        def fixed_qdq_u16(x):
            scale = 1.0 / 65536.0
            return jnp.clip(jnp.round(x / scale), 0.0, 65535.0) * scale

        def lpbq_dequant(w):
            O, I = w.shape
            qmax = 2.0 ** (W_BITS - 1) - 1.0
            wb = w.reshape(O, I // BLOCK, BLOCK)
            s = jnp.maximum(jnp.max(jnp.abs(wb), axis=-1, keepdims=True) / qmax, 1e-12)
            wq = jnp.clip(jnp.round(wb / s), -qmax - 1.0, qmax) * s
            return wq.reshape(O, I)
        x = act_qdq(x)
        up = act_qdq(x @ lpbq_dequant(w_up).T)
        gate = act_qdq(x @ lpbq_dequant(w_gate).T)
        sig = fixed_qdq_u16(jax.nn.sigmoid(gate))
        gate = act_qdq(gate * sig)
        o = act_qdq(gate * up)
        return o @ lpbq_dequant(w_down).T
    x = x + _L0_attn_ref(_layernorm(x, axis=-1), L0_attn_W_qkv)
    x = x + _L0_xattn_ref(_layernorm(x, axis=-1), ctx_1024, ctx_1024, mask_Bx1xS2_ik0, L0_xattn_Wq, L0_xattn_bq, L0_xattn_Wk, L0_xattn_bk, L0_xattn_Wv, L0_xattn_bv, L0_xattn_Wo, L0_xattn_bo)
    x = x + _L0_ffn_ref(_layernorm(x, axis=-1), L0_ffn_w_gate, L0_ffn_w_up, L0_ffn_w_down)
    return x

_drawn_inputs = setup_inputs


def setup_inputs(seed=0):
    import zlib

    import numpy as np

    out = dict(_drawn_inputs(seed))
    spreads = {}
    factors = {'L0_xattn_bk': 8.0, 'L0_ffn_w_gate': 6.418, 'L0_ffn_w_up': 6.285, 'L0_ffn_w_down': 6.323}
    for name, (base, spread) in spreads.items():
        noise = np.random.default_rng([zlib.crc32(name.encode()), seed]).standard_normal(out[name].shape)
        drawn = base * np.exp(spread * noise) if base else spread * noise
        out[name] = jnp.asarray(drawn.astype(out[name].dtype))
    for name, factor in factors.items():
        out[name] = (out[name] * factor).astype(out[name].dtype)
    return out
```

```python
from contextlib import ExitStack

import concourse.bass as bass
from concourse import mybir

ALU = mybir.AluOpType
ACT = mybir.ActivationFunctionType
F32 = mybir.dt.float32
F16 = mybir.dt.float16
BF16 = mybir.dt.bfloat16
I32 = mybir.dt.int32
I16 = mybir.dt.int16
U16 = mybir.dt.uint16
AX = mybir.AxisListType
RMAX = bass.bass_isa.ReduceOp.max

P = 128
B = 32
GB = 4
NG = B // GB
GT = GB * P
H = 16
DK = P // H
JT = 4
NSET = H // JT
RT = P // JT
FC = 3
QB = 32
EPS = 1e-5
MAGIC = 12582912.0
NEG = -1.0e9
CAUSAL = -1.0e30
BIG = 32768.0
AQ = 32767.0


def bc(ap, shape):
    return ap.broadcast_to(shape)


def decoder(nc, x, ctx_in, mask, Wqkv, Wq, bq, Wk, bk, Wv, bv, Wo, bo, w_gate, w_up, w_down, out):
    with ExitStack() as ctx:
        def sb(name, shape, dt=F32, where=ctx):
            return where.enter_context(nc.sbuf_tensor(name, shape, dt))

        def sem(name):
            return ctx.enter_context(nc.semaphore(name))

        X = sb("X", [P, B * P])
        ident = sb("ident", [P, P])
        identb = sb("identb", [P, P], BF16)
        zero_col = sb("zero_col", [P, 1])
        gateT = sb("gateT", [P, FC * P])
        upT = sb("upT", [P, FC * P])
        downT = sb("downT", [P, FC * P])
        stats = sb("stats", [P, 6 * B])
        mdif = sb("mdif", [P, B])
        msum = sb("msum", [P, B])
        mdq = sb("mdq", [P, B])
        sqs = sb("sqs", [P, B])
        mean = sb("mean", [P, B])
        vare = sb("vare", [P, B])
        rstd = sb("rstd", [P, B])
        mhalf = sb("mhalf", [P, B])
        X3 = sb("X3", [P, B * P])

        early = ExitStack()
        WS = sb("WS", [P, 3 * P], where=early)
        WX = sb("WX", [P, 4, P], where=early)
        WF = sb("WF", [P, 3, FC * P], where=early)
        WR = sb("WR", [P, 3 * FC * P], where=early)
        blkmax = sb("blkmax", [P, 36], where=early)
        blkscale = sb("blkscale", [P, 36], where=early)
        blkrecip = sb("blkrecip", [P, 36], where=early)
        WST = sb("WST", [P, 2 * P], where=early)
        A = sb("A", [P, P], where=early)
        WXT = sb("WXT", [P, 4, P], where=early)
        bcol = sb("bcol", [P, 3], where=early)
        borow = sb("borow", [1, P], where=early)
        bvrep = sb("bvrep", [P, P], where=early)
        cbias = sb("cbias", [P, P], where=early)
        ones = sb("ones", [P, P], where=early)
        causal = sb("causal", [P, P], where=early)
        M32 = sb("M32", [B, P], I32, where=early)
        M16 = sb("M16", [B, P], F16, where=early)
        MV = sb("MV", [B, P], where=early)
        vmask = sb("vmask", [P, B], where=early)
        anyv = sb("anyv", [P, B], where=early)
        bmask = sb("bmask", [P, B], where=early)
        mcol = sb("mcol", [P, 2, 2], where=early)
        sel8 = sb("sel8", [P, 4], where=early)
        sel8b = sb("sel8b", [P, 4], where=early)
        inj = sb("inj", [P, NSET, P], BF16, where=early)
        bigrow = sb("bigrow", [P, P], F16, where=early)
        sel0 = sb("sel0", [P, 1], where=early)
        onep = sb("onep", [P, JT, RT], where=early)
        ctxg = sb("ctxg", [P, GT], where=early)
        h = sb("h", [P, GT], where=early)
        hT = sb("hT", [P, GT], where=early)
        aT = sb("aT", [P, GT], where=early)
        v1 = sb("v1", [P, GT], where=early)
        sm = sb("sm", [P, GT], where=early)
        nmax = sb("nmax", [P, GB], where=early)
        pexp = sb("pexp", [P, GT], where=early)
        psum1 = sb("psum1", [P, GB], where=early)
        pinv = sb("pinv", [P, GB], where=early)
        pT = sb("pT", [P, GT], where=early)
        h2 = sb("h2", [P, GT], where=early)
        h2T = sb("h2T", [P, GT], where=early)
        cT = sb("cT", [P, GT], where=early)
        qhi = sb("qhi", [P, GT], F16, where=early)
        qlo = sb("qlo", [P, GT], F16, where=early)
        khi = sb("khi", [P, GT], F16, where=early)
        klo = sb("klo", [P, GT], F16, where=early)
        V2 = sb("V2", [P, B * P], where=early)
        qpack = sb("qpack", [P, 2, NSET, 2 * P], F16, where=early)
        kpack = sb("kpack", [P, 2, NSET, 2 * P], F16, where=early)
        mkey = sb("mkey", [P, 2, 2 * P], F16, where=early)
        VP = sb("VP", [P, 2, H, RT], where=early)
        PT = sb("PT", [P, 2, 2 * GT], where=early)
        nm = sb("nm", [P, H], where=early)
        NM = sb("NM", [P, JT, RT], BF16, where=early)
        mT = sb("mT", [P, P], BF16, where=early)
        osum = sb("osum", [P, P], where=early)
        oT = sb("oT", [P, P], where=early)
        early.close()

        late = ctx.enter_context(ExitStack())
        FW = FC * GT
        U = sb("U", [P, NG * FW], where=late)
        G = sb("G", [P, NG * FW], where=late)
        n3 = sb("n3", [P, GT], where=late)
        n3m = sb("n3m", [P, GT], where=late)
        n3T = sb("n3T", [P, GT], where=late)
        UN = sb("UN", [P, NG * FW], I16, where=late)
        ng = sb("ng", [P, 2, FW], I16, where=late)
        sig = sb("sig", [P, 2, FW], where=late)
        sq = sb("sq", [P, FW], U16, where=late)
        tn = sb("tn", [P, 2, FW], I16, where=late)
        on = sig
        y = sb("y", [P, 2, GT], where=late)
        mxs = sb("mxs", [P, 5, NG], where=late)
        mx1 = sb("mx1", [P, 5], where=late)
        mxa = sb("mxa", [P, 5], where=late)
        unit = sb("unit", [P, 5], where=late)
        sc0 = sb("sc0", [P, 5], where=late)
        scale = sb("scale", [P, 5], where=late)
        recip = sb("recip", [P, 5], where=late)
        lev = sb("lev", [P, 5], where=late)

        def dram(name, shape, dt):
            return nc.dram_tensor(name, shape, dt, kind="Internal").ap()

        q_dram = dram("q_dram", [NSET * JT, 4, DK, B * P], F16)
        k_dram = dram("k_dram", [NSET * JT, 4, DK, B * P], F16)
        m_dram = dram("m_dram", [B, P], F16)

        banks = ctx.enter_context(nc.psum_tensor("banks", [P, 8, GT], F32))

        def bank(n, k=1):
            return banks[:, n:n + k, :].rearrange("p k t -> p (k t)")

        names = """ld_w ld_x ld_ctx ld_m ld_wf
            c_set c_id c_causal c_wz c_sel8 c_inj c_sel0 c_big c_bcol c_bv
            w_t1 w_t1c w_a w_ac w_t2 w_t2c w_cb w_cbc
            m_cvt m_val m_t m_tc m_cnt m_any m_b0 m_b m_st
            f_max f_sc f_rc f_mul f_rnd f_sub f_clip f_deq f_t f_tc
            s_stat s_m1 s_m2 s_var s_rstd s_h s_hT s_hTc s_a s_ac s_v s_vc s_s s_sm s_nm s_exp s_pT s_pTc s_pv s_inv s_x1
            l_stat l_m1 l_m2 l_var l_rstd l_h l_hT l_hTc l_cT l_cTc l_k l_khi l_klo l_q l_qhi l_qlo l_v l_vc l_cb l_qst l_kst
            t_ld0 t_ld1 t_sn t_max t_nhi t_nm t_mT t_mTc t_st t_exp t_pv t_rec t_o t_wo t_x2 t_vp t_mk
            u_stat u_m1 u_m2 u_var u_rstd u_x3 u_mx
            g_mx g_all g_unit g_s0 g_s g_r g_lev
            a_rnd a_n3 a_nT a_nTc a_u a_uc a_mx
            b_ng b_sig b_sq b_t b_mx b_un c_tn c_o c_mx
            d_rnd d_on d_y d_yc d_st0 d_st1""".split()
        S = {n: sem(n) for n in names}

        block = ctx.enter_context(nc.Block())
        xs = x.rearrange("b s d -> s b d")
        cs = ctx_in.rearrange("b s d -> s b d")
        os = out.rearrange("b s d -> s b d")
        X4 = X[:, :].rearrange("p (b d) -> p b d", d=P)

        def copy_rows(d, c, g):
            return d[:, c, :, bass.ds(g * GT, GT)]

        def groups(eng, step):
            step(0)
            with eng.Fori(1, NG - 1) as g:
                step(g)
            step(NG - 1)

        def wait(eng, name, value):
            if not (isinstance(value, int) and value <= 0):
                eng.wait_ge(S[name], value)

        def first(g):
            return isinstance(g, int) and g == 0

        def last(g):
            return isinstance(g, int) and g == NG - 1

        def seq(t, g, b):
            return t[:, bass.ds(g * GT + b * P, P)]

        def grp(t, g, w=GT):
            return t[:, bass.ds(g * w, w)]

        @block.sync
        def _(sp):
            def load_context(g):
                sp.dma_start(ctxg[:, :].rearrange("p (b d) -> p b d", d=P),
                             cs[:, bass.ds(g * GB, GB), :]).then_inc(S["ld_ctx"], 16)

            sp.dma_start(WS[:, :], Wqkv).then_inc(S["ld_w"], 16)
            for n, w in enumerate((Wq, Wk, Wv, Wo)):
                sp.dma_start(WX[:, n, :], w).then_inc(S["ld_w"], 16)
            for n, b_ in enumerate((bq, bk, bv)):
                sp.dma_start(bcol[:, n:n + 1], b_.rearrange("(p o) -> p o", o=1)).then_inc(S["ld_w"], 16)
            sp.dma_start(borow[:, :], bo.rearrange("(o d) -> o d", o=1)).then_inc(S["ld_w"], 16)
            sp.dma_start(M32[:, :], mask.rearrange("b o s -> (b o) s")).then_inc(S["ld_m"], 16)
            for q in range(4):
                r = slice(q * B // 4, (q + 1) * B // 4)
                sp.dma_start(X4[:, r, :], xs[:, r, :]).then_inc(S["ld_x"], 16)
            load_context(0)
            for n, w in enumerate((w_gate, w_up)):
                sp.dma_start(WF[:, n, :].rearrange("p (c d) -> p c d", c=FC),
                             w.rearrange("(c p) d -> p c d", c=FC)).then_inc(S["ld_wf"], 16)
            sp.dma_start(WF[:, 2, :], w_down).then_inc(S["ld_wf"], 16)
            sp.wait_ge(S["m_cvt"], 1)
            sp.dma_start(m_dram, M16[:, :]).then_inc(S["m_st"], 16)

            def store(g):
                sp.wait_ge(S["l_klo"], g + 1)
                for c in range(4):
                    sp.dma_start(copy_rows(k_dram, c, g), (khi, klo)[c % 2][:, :]).then_inc(S["l_kst"], 16)
                sp.wait_ge(S["l_qlo"], g + 1)
                for c in range(4):
                    sp.dma_start(copy_rows(q_dram, c, g), (qhi, qlo)[c // 2][:, :]).then_inc(S["l_qst"], 16)

            def store_and_load(g):
                sp.wait_ge(S["l_cT"], g + 1)
                load_context(g + 1)
                store(g)

            with sp.Fori(0, NG - 1) as g:
                store_and_load(g)
            store(NG - 1)

            sp.wait_ge(S["l_kst"], 64 * NG)
            sp.wait_ge(S["l_qst"], 64 * NG)

            def fill(slot, t0):
                sp.wait_ge(S["m_st"], 16)
                for d, t in ((q_dram, qpack), (k_dram, kpack)):
                    src = d.rearrange("(s j) c e t -> (j c e) s t", s=NSET)
                    sp.dma_start(t[:, slot], src[:, :, bass.ds(t0, 2 * P)]).then_inc(S["t_ld%d" % slot], 16)
                flat = m_dram.rearrange("b s -> (b s)")
                sp.dma_start(mkey[:, slot], flat[bass.ds(t0, 2 * P)].partition_broadcast(P)).then_inc(S["t_ld%d" % slot], 16)

            fill(0, 0)

            def fill_second(g):
                wait(sp, "t_st", 8 * g)
                fill(1, g * GT + 2 * P)

            def fill_both(g):
                fill_second(g)
                sp.wait_ge(S["t_st"], 8 * g + 4)
                fill(0, g * GT + GT)

            fill_both(0)
            with sp.Fori(1, NG - 1) as g:
                fill_both(g)
            fill_second(NG - 1)

            with sp.Fori(0, NG // 2) as i:
                for u in range(2):
                    sp.wait_ge(S["d_yc"], 2 * i + u + 1)
                    sp.dma_start(os[:, bass.ds(i * 2 * GB + u * GB, GB), :],
                                 y[:, u].rearrange("p (b d) -> p b d", d=P)).then_inc(S["d_st%d" % u], 16)
            sp.wait_ge(S["d_st0"], 16 * NG // 2)
            sp.wait_ge(S["d_st1"], 16 * NG // 2)

        @block.gpsimd
        def _(pool):
            nc.gpsimd.memset(ident[:, :], 0.0).then_inc(S["c_set"], 1)
            nc.gpsimd.memset(causal[:, :], 0.0).then_inc(S["c_set"], 1)
            nc.gpsimd.memset(mhalf[:, :], -0.5).then_inc(S["c_set"], 1)
            pool.wait_ge(S["c_set"], 3)
            nc.gpsimd.affine_select(out=ident[:, :], in_=ident[:, :], compare_op=ALU.not_equal, fill=1.0,
                                    base=0, pattern=[[-1, P]], channel_multiplier=1).then_inc(S["c_id"], 1)
            nc.gpsimd.affine_select(out=causal[:, :], in_=causal[:, :], compare_op=ALU.is_ge, fill=CAUSAL,
                                    base=0, pattern=[[-1, P]], channel_multiplier=1).then_inc(S["c_causal"], 1)
            pool.wait_ge(S["s_var"], 1)
            nc.gpsimd.tensor_tensor(rstd[:, :], vare[:, :], mhalf[:, :], ALU.pow).then_inc(S["s_rstd"], 1)

            pool.wait_ge(S["f_rc"], 1)
            W3 = WF[:, :, :].rearrange("p m (k e) -> p (m k) e", e=QB)
            R3 = WR[:, :].rearrange("p (k e) -> p k e", e=QB)
            wide = [P, 3 * FC * P // QB, QB]
            WR1 = WR[:, :]
            nc.gpsimd.tensor_tensor(R3, W3, bc(blkrecip[:, :].unsqueeze(2), wide), ALU.mult).then_inc(S["f_mul"], 1)
            pool.wait_ge(S["f_mul"], 1)
            nc.gpsimd.tensor_scalar(WR1, WR1, MAGIC, None, ALU.add).then_inc(S["f_rnd"], 1)
            pool.wait_ge(S["f_rnd"], 1)
            nc.gpsimd.tensor_scalar(WR1, WR1, -MAGIC, None, ALU.add).then_inc(S["f_sub"], 1)
            pool.wait_ge(S["f_sub"], 1)
            nc.gpsimd.tensor_scalar(WR1, WR1, 7.0, -8.0, ALU.min, ALU.max).then_inc(S["f_clip"], 1)
            pool.wait_ge(S["f_clip"], 1)
            nc.gpsimd.tensor_tensor(R3, R3, bc(blkscale[:, :].unsqueeze(2), wide), ALU.mult).then_inc(S["f_deq"], 1)

            with pool.Fori(0, NG) as g:
                pool.wait_ge(S["l_var"], g + 1)
                nc.gpsimd.tensor_tensor(rstd[:, bass.ds(g * GB, GB)], vare[:, bass.ds(g * GB, GB)],
                                        mhalf[:, 0:GB], ALU.pow).then_inc(S["l_rstd"], 1)
                pool.wait_ge(S["l_h"], GB * g + GB)
                pool.wait_ge(S["w_cbc"], 1)
                xg = grp(X, g).rearrange("p (b d) -> p b d", d=P)
                nc.gpsimd.tensor_tensor(xg, xg, bc(cbias[:, :].unsqueeze(1), [P, GB, P]), ALU.add).then_inc(S["l_cb"], 1)

            pool.wait_ge(S["l_vc"], NG)
            pool.wait_ge(S["c_wz"], 6)
            pool.wait_ge(S["m_b"], 1)

            def values(g):
                for b in range(GB):
                    if not (first(g) and b < 2):
                        pool.wait_ge(S["t_pv"], 2 * GB * g + 2 * b - 2)
                    nc.gpsimd.tensor_copy(mcol[:, b % 2, 0:1], vmask[:, bass.ds(GB * g + b, 1)]).then_inc(S["t_mk"], 1)
                    nc.gpsimd.tensor_copy(mcol[:, b % 2, 1:2], bmask[:, bass.ds(GB * g + b, 1)]).then_inc(S["t_mk"], 1)
                    src = seq(V2, g, b).rearrange("p (s j e) -> p s j e", s=NSET, j=JT)
                    dst = VP[:, b % 2].rearrange("p (s j) c -> p s j c", j=JT)
                    for j in range(JT):
                        nc.gpsimd.tensor_copy(dst[:, :, j, DK * j:DK * j + DK], src[:, :, j, :]).then_inc(S["t_vp"], 1)

            groups(pool, values)

            pool.wait_ge(S["u_var"], 1)
            nc.gpsimd.tensor_tensor(rstd[:, :], vare[:, :], mhalf[:, :], ALU.pow).then_inc(S["u_rstd"], 1)
            for n, (k0, k1) in enumerate(((0, 1), (1, 3), (3, 4), (4, 5))):
                pool.wait_ge(S["g_mx"], n + 1)
                nc.gpsimd.partition_all_reduce(mxa[:, k0:k1], mx1[:, k0:k1], P, RMAX).then_inc(S["g_all"], 1)

        @block.tensor
        def _(pe):
            pe.wait_ge(S["c_id"], 1)
            pe.wait_ge(S["ld_w"], 16 * 9)
            pe.transpose(bank(0)[:, 0:P], WS[:, 0:P], ident[:, :])
            pe.transpose(bank(0)[:, P:2 * P], WS[:, P:2 * P], ident[:, :]).then_inc(S["w_t1"], 1)
            for n in range(4):
                m = pe.transpose(bank(2)[:, n * P:(n + 1) * P], WX[:, n, :], ident[:, :])
            m.then_inc(S["w_t2"], 1)
            pe.wait_ge(S["w_t1c"], 1)
            pe.matmul(bank(1)[:, 0:P], WST[:, 0:P], WST[:, P:2 * P], start=True, stop=True).then_inc(S["w_a"], 1)
            pe.wait_ge(S["w_t2c"], 2)
            pe.wait_ge(S["c_bv"], 1)
            pe.wait_ge(S["c_wz"], 1)
            pe.matmul(bank(3)[:, 0:P], bvrep[:, :], WXT[:, 3, :], start=True, stop=False)
            pe.matmul(bank(3)[:, 0:P], ones[0:1, :], borow[:, :], start=False, stop=True).then_inc(S["w_cb"], 1)
            pe.wait_ge(S["m_val"], 1)
            pe.transpose(bank(4)[:, 0:B], MV[:, :], ident[0:B, 0:B]).then_inc(S["m_t"], 1)
            pe.wait_ge(S["m_tc"], 1)
            pe.matmul(bank(5)[:, 0:B], ones[:, :], vmask[:, :], start=True, stop=True).then_inc(S["m_cnt"], 1)
            pe.wait_ge(S["w_ac"], 1)
            pe.wait_ge(S["w_cbc"], 1)
            pe.wait_ge(S["m_b"], 1)

            def transposes(n, src):
                for b in range(GB):
                    m = pe.transpose(bank(n)[:, b * P:(b + 1) * P], src(b), ident[:, :])
                return m

            def step(cur, nxt):
                if cur is not None:
                    pe.wait_ge(S["s_exp"], GB * cur + GB)
                    wait(pe, "l_hTc", cur)
                    transposes(5, lambda b: pexp[:, b * P:(b + 1) * P]).then_inc(S["s_pT"], 1)
                if nxt is not None:
                    pe.wait_ge(S["s_h"], GB * nxt + GB)
                    wait(pe, "s_hTc", nxt)
                    transposes(0, lambda b: h[:, b * P:(b + 1) * P]).then_inc(S["s_hT"], 1)
                if cur is not None:
                    pe.wait_ge(S["ld_ctx"], 16 * cur + 16)
                    wait(pe, "l_vc", cur)
                    transposes(1, lambda b: ctxg[:, b * P:(b + 1) * P]).then_inc(S["l_cT"], 1)
                    pe.wait_ge(S["s_pTc"], cur + 1)
                    pe.wait_ge(S["s_vc"], cur + 1)
                    wait(pe, "l_qlo", cur)
                    for b in range(GB):
                        r = slice(b * P, (b + 1) * P)
                        m = pe.matmul(bank(6)[:, r], pT[:, r], v1[:, r], start=True, stop=True)
                    m.then_inc(S["s_pv"], 1)
                if nxt is not None:
                    pe.wait_ge(S["s_hTc"], nxt + 1)
                    wait(pe, "s_ac", nxt)
                    pe.matmul(bank(2), A[:, :], hT[:, :], start=True, stop=True).then_inc(S["s_a"], 1)
                    wait(pe, "s_vc", nxt)
                    for b in range(GB):
                        r = slice(b * P, (b + 1) * P)
                        m = pe.matmul(bank(3)[:, r], hT[:, r], WS[:, 2 * P:3 * P], start=True, stop=True)
                    m.then_inc(S["s_v"], 1)
                if cur is not None:
                    pe.wait_ge(S["l_cTc"], cur + 1)
                    wait(pe, "l_klo", cur)
                    pe.matmul(bank(7), WXT[:, 1, :], cT[:, :], start=True, stop=True).then_inc(S["l_k"], 1)
                if nxt is not None:
                    pe.wait_ge(S["s_ac"], nxt + 1)
                    wait(pe, "s_sm", nxt)
                    for b in range(GB):
                        r = slice(b * P, (b + 1) * P)
                        m = pe.matmul(bank(4)[:, r], aT[:, r], hT[:, r], start=True, stop=True)
                    m.then_inc(S["s_s"], 1)
                if cur is not None:
                    for b in range(GB):
                        r = slice(b * P, (b + 1) * P)
                        m = pe.matmul(bank(1)[:, r], cT[:, r], WXT[:, 2, :], start=True, stop=True)
                    m.then_inc(S["l_v"], 1)
                    pe.wait_ge(S["l_h"], GB * cur + GB)
                    transposes(5, lambda b: h2[:, b * P:(b + 1) * P]).then_inc(S["l_hT"], 1)
                    pe.wait_ge(S["l_hTc"], cur + 1)
                    pe.wait_ge(S["s_x1"], GB * cur + GB)
                    pe.matmul(bank(6), WXT[:, 0, :], h2T[:, :], start=True, stop=True).then_inc(S["l_q"], 1)

            step(None, 0)
            step(0, 1)
            with pe.Fori(1, NG - 1) as g:
                step(g, g + 1)
            step(NG - 1, None)

            pe.wait_ge(S["f_deq"], 1)
            pe.wait_ge(S["s_hTc"], NG)
            pe.wait_ge(S["l_vc"], NG)
            for m_ in range(3):
                for c in range(FC):
                    w = WR[:, m_ * FC * P + c * P:m_ * FC * P + (c + 1) * P]
                    m = pe.transpose(bank(m_)[:, c * P:(c + 1) * P], w, ident[:, :])
            m.then_inc(S["f_t"], 1)
            pe.wait_ge(S["f_tc"], 3)
            pe.wait_ge(S["l_qlo"], NG)
            pe.wait_ge(S["l_klo"], NG)
            pe.wait_ge(S["l_hTc"], NG)
            pe.wait_ge(S["c_big"], 1)
            pe.wait_ge(S["c_inj"], 1)

            def rows(j):
                return slice(RT * j, RT * j + RT)

            def scores_q(nxt, p, b):
                pe.wait_ge(S["t_max"], 2 * nxt + p)
                slot, t = (b // 2) % 2, slice(b % 2 * P, b % 2 * P + P)
                for jj in range(2):
                    r = rows(2 * p + jj)
                    pe.matmul(bank(jj), bigrow[r, :], bc(mkey[r, slot, t].unsqueeze(1), [RT, NSET, P]),
                              start=True, stop=False, skip_group_check=True)
                for s in range(NSET):
                    for jj in range(2):
                        r = rows(2 * p + jj)
                        m = pe.matmul(bank(jj)[:, s * P:(s + 1) * P], qpack[r, slot, s, t], kpack[r, slot, s, t],
                                      start=False, stop=(s == NSET - 1), skip_group_check=True)
                m.then_inc(S["t_sn"], 1)

            def scores_k(cur, p, b):
                slot, t = (b // 2) % 2, slice(b % 2 * P, b % 2 * P + P)
                for s in range(NSET):
                    for jj in range(2):
                        r = rows(2 * p + jj)
                        pe.matmul(bank(2 + jj)[:, s * P:(s + 1) * P], kpack[r, slot, s, t], qpack[r, slot, s, t],
                                  start=(s == 0), stop=False, skip_group_check=True)
                for s in range(NSET):
                    for jj in range(2):
                        r = rows(2 * p + jj)
                        m = pe.matmul(bank(2 + jj)[:, s * P:(s + 1) * P], inj[r, s, :], mT[r, :],
                                      start=False, stop=(s == NSET - 1), skip_group_check=True)
                m.then_inc(S["t_st"], 1)

            def pv(p, b):
                for jj in range(2):
                    j = 2 * p + jj
                    for s in range(NSET):
                        pe.matmul(bank(4 + b % 2)[RT * s:RT * s + RT, 0:P], VP[:, b % 2, JT * s + j, :],
                                  PT[:, p, (jj * NSET + s) * P:(jj * NSET + s + 1) * P],
                                  start=(j == 0), stop=(j == JT - 1), skip_group_check=True,
                                  tile_position=(0, RT * s))
                    for s in range(NSET):
                        m = pe.matmul(bank(4 + b % 2)[RT * s:RT * s + RT, P:2 * P], onep[:, j, :],
                                      PT[:, p, (jj * NSET + s) * P:(jj * NSET + s + 1) * P],
                                      start=False, stop=(j == JT - 1), skip_group_check=True,
                                      tile_position=(0, RT * s))
                m.then_inc(S["t_pv"], 1)

            def max_rows(nxt):
                pe.wait_ge(S["t_nm"], nxt + 1)
                wait(pe, "t_mTc", nxt)
                pe.transpose(bank(7).bitcast(BF16)[:, 0:P], NM[:, :, :].rearrange("p j r -> p (j r)"),
                             identb[:, :]).then_inc(S["t_mT"], 1)

            def project(prev, skip=False):
                pe.wait_ge(S["t_o"], prev + 1)
                if not skip:
                    wait(pe, "t_x2", prev)
                pe.matmul(bank(6)[:, 0:P], oT[:, :], WXT[:, 3, :], start=True, stop=True).then_inc(S["t_wo"], 1)

            def cross(g):
                for b in range(GB):
                    cur = GB * g + b
                    more = not (last(g) and b == GB - 1)
                    begun = not (first(g) and b == 0)
                    if more:
                        if b % 2:
                            pe.wait_ge(S["t_ld1" if b == 1 else "t_ld0"], 48 * g + (48 if b == 1 else 96))
                        scores_q(cur + 1, 0, b + 1)
                    pe.wait_ge(S["t_mTc"], cur + 1)
                    wait(pe, "t_exp", 2 * cur)
                    scores_k(cur, 0, b)
                    if begun:
                        pv(1, b - 1)
                    if more:
                        scores_q(cur + 1, 1, b + 1)
                    pe.wait_ge(S["t_exp"], 2 * cur + 1)
                    scores_k(cur, 1, b)
                    if begun:
                        project(cur - 1)
                    pe.wait_ge(S["t_vp"], JT * cur + JT)
                    if not (first(g) and b < 2):
                        wait(pe, "t_o", cur - 1)
                    pv(0, b)
                    if more:
                        max_rows(cur + 1)

            pe.wait_ge(S["t_ld0"], 48)
            scores_q(0, 0, 0)
            scores_q(0, 1, 0)
            max_rows(0)
            groups(pe, cross)
            pe.wait_ge(S["t_exp"], 2 * B)
            pv(1, B - 1)
            project(B - 1)

            def up_gate(g):
                pe.wait_ge(S["a_n3"], g + 1)
                if not first(g):
                    wait(pe, "a_nTc", g)
                transposes(0, lambda b: n3[:, b * P:(b + 1) * P]).then_inc(S["a_nT"], 1)
                pe.wait_ge(S["a_nTc"], g + 1)
                for k in range(6):
                    if not first(g):
                        pe.wait_ge(S["a_uc"], 6 * g - 5 + k)
                    w = (upT, gateT)[k // FC]
                    pe.matmul(bank(2 + k), w[:, k % FC * P:k % FC * P + P], n3T[:, :],
                              start=True, stop=True).then_inc(S["a_u"], 1)

            pe.wait_ge(S["t_x2"], B)
            groups(pe, up_gate)

            def down(i, u, begun):
                g = 2 * i + u
                pe.wait_ge(S["d_on"], g + 1)
                if begun:
                    pe.wait_ge(S["d_yc"], g - 1)
                for b in range(GB):
                    for c in range(FC):
                        m = pe.matmul(bank(u)[:, b * P:(b + 1) * P], on[:, u, c * GT + b * P:c * GT + b * P + P],
                                      downT[:, c * P:(c + 1) * P], start=(c == 0), stop=(c == FC - 1))
                m.then_inc(S["d_y"], 1)

            down(0, 0, False)
            down(0, 1, False)
            with pe.Fori(1, NG // 2) as i:
                down(i, 0, True)
                down(i, 1, True)

        @block.scalar
        def _(act):
            act.preload_act_table(ACT.Exp)
            act.wait_ge(S["w_t1"], 1)
            act.activation(WST[:, :], bank(0)[:, 0:2 * P], ACT.Copy).then_inc(S["w_t1c"], 1)
            act.wait_ge(S["w_t2"], 1)
            act.activation(WXT[:, 0, :], bank(2)[:, 0:P], ACT.Copy, scale=float(DK) ** -0.5).then_inc(S["w_t2c"], 1)
            act.activation(WXT[:, 1:4, :].rearrange("p n d -> p (n d)"), bank(2)[:, P:4 * P], ACT.Copy).then_inc(S["w_t2c"], 1)
            act.wait_ge(S["w_a"], 1)
            act.activation(A[:, :], bank(1)[:, 0:P], ACT.Copy, scale=float(P) ** -0.5).then_inc(S["w_ac"], 1)
            act.wait_ge(S["c_bcol"], 1)

            def step(cur, nxt):
                if nxt is not None:
                    act.wait_ge(S["s_hT"], nxt + 1)
                    wait(act, "s_s", nxt)
                    act.activation(hT[:, :], bank(0), ACT.Copy).then_inc(S["s_hTc"], 1)
                if cur is not None:
                    act.wait_ge(S["l_cT"], cur + 1)
                    wait(act, "l_v", cur)
                    act.activation(cT[:, :], bank(1), ACT.Copy).then_inc(S["l_cTc"], 1)
                if nxt is not None:
                    act.wait_ge(S["s_a"], nxt + 1)
                    act.activation(aT[:, :], bank(2), ACT.Copy).then_inc(S["s_ac"], 1)
                    act.wait_ge(S["s_v"], nxt + 1)
                    wait(act, "s_pv", nxt)
                    act.activation(v1[:, :], bank(3), ACT.Copy).then_inc(S["s_vc"], 1)
                if cur is not None:
                    act.wait_ge(S["l_k"], cur + 1)
                    wait(act, "l_kst", 64 * cur)
                    act.activation(khi[:, :], bank(7), ACT.Identity, bias=bcol[:, 1:2]).then_inc(S["l_khi"], 1)
                    act.wait_ge(S["l_v"], cur + 1)
                    act.activation(grp(V2, cur), bank(1), ACT.Copy).then_inc(S["l_vc"], 1)
                if nxt is not None:
                    act.wait_ge(S["s_nm"], nxt + 1)
                    wait(act, "s_pT", nxt)
                    wait(act, "s_inv", nxt)
                    for b in range(GB):
                        r = slice(b * P, (b + 1) * P)
                        act.activation(pexp[:, r], sm[:, r], ACT.Exp, bias=nmax[:, b:b + 1],
                                       accum_out=psum1[:, b:b + 1]).then_inc(S["s_exp"], 1)
                if cur is not None:
                    act.wait_ge(S["l_hT"], cur + 1)
                    wait(act, "l_q", cur)
                    act.activation(h2T[:, :], bank(5), ACT.Copy).then_inc(S["l_hTc"], 1)
                    act.wait_ge(S["l_q"], cur + 1)
                    wait(act, "l_qst", 64 * cur)
                    act.activation(qhi[:, :], bank(6), ACT.Identity, bias=bcol[:, 0:1]).then_inc(S["l_qhi"], 1)

            step(None, 0)
            step(0, 1)
            with act.Fori(1, NG - 1) as g:
                step(g, g + 1)
            step(NG - 1, None)

            act.wait_ge(S["f_t"], 1)
            for n, w in enumerate((gateT, upT, downT)):
                act.activation(w[:, :], bank(n)[:, 0:FC * P], ACT.Copy).then_inc(S["f_tc"], 1)


            def probs(g):
                for b in range(GB):
                    for p in range(2):
                        n = 2 * GB * g + 2 * b + p
                        act.wait_ge(S["t_st"], n + 1)
                        if not (first(g) and b == 0):
                            act.wait_ge(S["t_pv"], n - 1)
                        if p == 0:
                            act.wait_ge(S["t_mk"], 2 * GB * g + 2 * b + 2)
                        act.activation(PT[:, p, :], bank(2, 2), ACT.Exp, bias=mcol[:, b % 2, 1:2],
                                       scale=mcol[:, b % 2, 0:1]).then_inc(S["t_exp"], 1)

            groups(act, probs)

            act.wait_ge(S["t_x2"], B)

            def up_gate(g):
                act.wait_ge(S["a_nT"], g + 1)
                if not first(g):
                    act.wait_ge(S["a_u"], 6 * g)
                act.activation(n3T[:, :], bank(0), ACT.Copy).then_inc(S["a_nTc"], 1)
                for k in range(6):
                    act.wait_ge(S["a_u"], 6 * g + k + 1)
                    act.activation((U, G)[k // FC][:, bass.ds(g * FW + k % FC * GT, GT)], bank(2 + k),
                                   ACT.Copy).then_inc(S["a_uc"], 1)

            groups(act, up_gate)

            act.wait_ge(S["g_lev"], 2)
            act.preload_act_table(ACT.Sigmoid)

            def gate(i, u, begun):
                g = 2 * i + u
                if begun:
                    act.wait_ge(S["b_t"], g - 1)
                act.activation(ng[:, u], grp(G, g, FW), ACT.Copy, scale=lev[:, 2:3]).then_inc(S["b_ng"], 1)
                act.activation(grp(UN, g, FW), grp(U, g, FW), ACT.Copy, scale=lev[:, 1:2]).then_inc(S["b_un"], 1)
                act.wait_ge(S["b_ng"], g + 1)
                if begun:
                    act.wait_ge(S["b_sq"], g - 1)
                act.activation(sig[:, u], ng[:, u], ACT.Sigmoid, scale=scale[:, 2:3]).then_inc(S["b_sig"], 1)

            def pairs(step):
                step(0, 0, False)
                step(0, 1, False)
                with act.Fori(1, NG // 2) as i:
                    step(i, 0, True)
                    step(i, 1, True)

            pairs(gate)

            act.wait_ge(S["g_lev"], 3)

            def gated(i, u, begun):
                g = 2 * i + u
                if begun:
                    act.wait_ge(S["c_o"], g - 1)
                act.activation(tn[:, u], grp(G, g, FW), ACT.Copy, scale=lev[:, 3:4]).then_inc(S["c_tn"], 1)

            pairs(gated)

        @block.vector
        def _(dve):
            V = nc.vector
            V.memset(ones[:, :], 1.0).then_inc(S["c_wz"], 1)
            V.memset(zero_col[:, :], 0.0).then_inc(S["c_wz"], 1)
            V.memset(VP[:, :, :, :], 0.0).then_inc(S["c_wz"], 1)
            V.memset(NM[:, :, :], 0.0).then_inc(S["c_wz"], 1)
            V.memset(onep[:, :, :], 0.0).then_inc(S["c_wz"], 1)
            dve.wait_ge(S["c_wz"], 5)
            for j in range(JT):
                m = V.memset(onep[:, j, DK * j:DK * j + DK], 1.0)
            m.then_inc(S["c_wz"], 1)
            dve.wait_ge(S["c_id"], 1)
            V.tensor_copy(identb[:, :], ident[:, :]).then_inc(S["c_wz"], 1)
            iv = ident[:, :].rearrange("p (j r) -> p r j", j=JT)
            V.tensor_reduce(sel8[:, 0:4], iv[:, 0:4, :], AX.X, ALU.add).then_inc(S["c_sel8"], 1)
            V.tensor_reduce(sel8b[:, 0:4], iv[:, 4:8, :], AX.X, ALU.add).then_inc(S["c_sel8"], 1)
            V.tensor_reduce(sel0[:, :], iv[:, 0:1, :], AX.X, ALU.add).then_inc(S["c_sel0"], 1)
            dve.wait_ge(S["c_sel8"], 2)
            V.tensor_tensor(sel8[:, :], sel8[:, :], sel8b[:, :], ALU.add).then_inc(S["c_sel8"], 1)
            dve.wait_ge(S["c_sel8"], 3)
            V.tensor_copy(inj[:, :, :], bc(sel8[:, :].unsqueeze(2), [P, NSET, P])).then_inc(S["c_inj"], 1)
            dve.wait_ge(S["c_sel0"], 1)
            V.tensor_scalar(bigrow[:, :], bc(sel0[:, :], [P, P]), BIG, None, ALU.mult).then_inc(S["c_big"], 1)
            dve.wait_ge(S["ld_w"], 16 * 9)
            V.tensor_scalar(bcol[:, 0:1], bcol[:, 0:1], float(DK) ** -0.5, None, ALU.mult).then_inc(S["c_bcol"], 1)
            V.tensor_scalar(bvrep[:, :], ones[:, :], bcol[:, 2:3], None, ALU.mult).then_inc(S["c_bv"], 1)
            dve.wait_ge(S["ld_m"], 16)
            V.tensor_scalar(M16[:, :], M32[:, :], 0.0, -BIG, ALU.is_equal, ALU.mult).then_inc(S["m_cvt"], 1)
            V.tensor_scalar(MV[:, :], M32[:, :], 0.0, None, ALU.not_equal).then_inc(S["m_val"], 1)
            dve.wait_ge(S["m_t"], 1)
            V.tensor_copy(vmask[:, :], bank(4)[:, 0:B]).then_inc(S["m_tc"], 1)
            dve.wait_ge(S["m_cnt"], 1)
            V.tensor_scalar(anyv[:, :], bank(5)[:, 0:B], 1.0, -NEG, ALU.min, ALU.mult).then_inc(S["m_any"], 1)
            dve.wait_ge(S["m_any"], 1)
            V.scalar_tensor_tensor(out=bmask[:, :], in0=vmask[:, :], scalar=-1.0, in1=anyv[:, :],
                                   op0=ALU.add, op1=ALU.mult).then_inc(S["m_b"], 1)
            dve.wait_ge(S["w_cb"], 1)
            V.tensor_copy(cbias[:, :], bank(3)[:, 0:P]).then_inc(S["w_cbc"], 1)
            dve.wait_ge(S["ld_wf"], 48)
            V.tensor_reduce(blkmax[:, :], WF[:, :, :].rearrange("p m (k e) -> p (m k) e", e=QB), AX.X, ALU.max,
                            apply_absolute_value=True).then_inc(S["f_max"], 1)
            dve.wait_ge(S["f_max"], 1)
            V.tensor_scalar(blkscale[:, :], blkmax[:, :], 1.0 / 7.0, 1e-12, ALU.mult, ALU.max).then_inc(S["f_sc"], 1)
            dve.wait_ge(S["f_sc"], 1)
            V.reciprocal(blkrecip[:, :], blkscale[:, :]).then_inc(S["f_rc"], 1)

            def stat(t, g, b, s):
                V.bn_stats(stats[:, bass.ds(6 * (GB * g + b), 6)], seq(t, g, b)).then_inc(s, 1)

            even_odd = stats[:, :].rearrange("p (b f) -> p b f", f=6)

            def moments(b0, n, s_1, s_2, s_3, done1, done2):
                r, q = bass.ds(b0, n), bass.ds(b0, n)
                me, mo = even_odd[:, r, 1], even_odd[:, r, 4]
                V.tensor_tensor(mdif[:, q], me, mo, ALU.subtract).then_inc(s_1, 1)
                V.tensor_tensor(msum[:, q], me, mo, ALU.add).then_inc(s_1, 1)
                V.scalar_tensor_tensor(out=sqs[:, q], in0=even_odd[:, r, 2], scalar=P * EPS, in1=even_odd[:, r, 5],
                                       op0=ALU.add, op1=ALU.add).then_inc(s_1, 1)
                dve.wait_ge(s_1, done1)
                V.tensor_scalar(mean[:, q], msum[:, q], 0.5, None, ALU.mult).then_inc(s_2, 1)
                V.scalar_tensor_tensor(out=mdq[:, q], in0=mdif[:, q], scalar=0.25, in1=mdif[:, q],
                                       op0=ALU.mult, op1=ALU.mult).then_inc(s_2, 1)
                dve.wait_ge(s_2, done2)
                V.scalar_tensor_tensor(out=vare[:, q], in0=sqs[:, q], scalar=1.0 / P, in1=mdq[:, q],
                                       op0=ALU.mult, op1=ALU.add).then_inc(s_3, 1)

            dve.wait_ge(S["ld_x"], 64)
            with dve.Fori(0, NG) as g:
                for b in range(GB):
                    stat(X, g, b, S["s_stat"])
            dve.wait_ge(S["s_stat"], B)
            moments(0, B, S["s_m1"], S["s_m2"], S["s_var"], 3, 2)
            dve.wait_ge(S["s_m2"], 2)
            dve.wait_ge(S["s_rstd"], 1)
            dve.wait_ge(S["c_causal"], 1)

            def normalise(dst, src, g, b):
                return V.tensor_scalar(dst, src, mean[:, bass.ds(GB * g + b, 1)], rstd[:, bass.ds(GB * g + b, 1)],
                                       ALU.subtract, ALU.mult)

            def step(cur, nxt):
                if nxt is not None:
                    wait(dve, "s_hT", nxt)
                    for b in range(GB):
                        normalise(h[:, b * P:(b + 1) * P], seq(X, nxt, b), nxt, b).then_inc(S["s_h"], 1)
                if cur is not None:
                    dve.wait_ge(S["s_pT"], cur + 1)
                    wait(dve, "s_pv", cur)
                    V.tensor_copy(pT[:, :], bank(5)).then_inc(S["s_pTc"], 1)
                    wait(dve, "s_x1", GB * cur)
                    V.reciprocal(pinv[:, :], psum1[:, :]).then_inc(S["s_inv"], 1)
                    dve.wait_ge(S["s_pv"], cur + 1)
                    dve.wait_ge(S["s_inv"], cur + 1)
                    for b in range(GB):
                        V.scalar_tensor_tensor(out=seq(X, cur, b), in0=bank(6)[:, b * P:(b + 1) * P],
                                               scalar=pinv[:, b:b + 1], in1=seq(X, cur, b),
                                               op0=ALU.mult, op1=ALU.add).then_inc(S["s_x1"], 1)
                    dve.wait_ge(S["s_x1"], GB * cur + GB)
                    for b in range(GB):
                        stat(X, cur, b, S["l_stat"])
                    dve.wait_ge(S["l_stat"], GB * cur + GB)
                    moments(GB * cur, GB, S["l_m1"], S["l_m2"], S["l_var"], 3 * cur + 3, 2 * cur + 2)
                if nxt is not None:
                    dve.wait_ge(S["s_s"], nxt + 1)
                    wait(dve, "s_exp", GB * nxt)
                    V.tensor_tensor(sm[:, :].rearrange("p (b m) -> p b m", m=P),
                                    bank(4).rearrange("p (b m) -> p b m", m=P),
                                    bc(causal[:, :].unsqueeze(1), [P, GB, P]), ALU.add).then_inc(S["s_sm"], 1)
                    dve.wait_ge(S["s_sm"], nxt + 1)
                    V.tensor_reduce(nmax[:, :], sm[:, :].rearrange("p (b m) -> p b m", m=P), AX.X, ALU.max,
                                    negate=True).then_inc(S["s_nm"], 1)
                if cur is not None:
                    dve.wait_ge(S["l_khi"], cur + 1)
                    wait(dve, "l_kst", 64 * cur)
                    V.scalar_tensor_tensor(out=klo[:, :], in0=bank(7), scalar=bcol[:, 1:2], in1=khi[:, :],
                                           op0=ALU.add, op1=ALU.subtract).then_inc(S["l_klo"], 1)
                    dve.wait_ge(S["l_rstd"], cur + 1)
                    wait(dve, "l_hT", cur)
                    for b in range(GB):
                        normalise(h2[:, b * P:(b + 1) * P], seq(X, cur, b), cur, b).then_inc(S["l_h"], 1)
                    dve.wait_ge(S["l_qhi"], cur + 1)
                    wait(dve, "l_qst", 64 * cur)
                    V.scalar_tensor_tensor(out=qlo[:, :], in0=bank(6), scalar=bcol[:, 0:1], in1=qhi[:, :],
                                           op0=ALU.add, op1=ALU.subtract).then_inc(S["l_qlo"], 1)

            step(None, 0)
            step(0, 1)
            with dve.Fori(1, NG - 1) as g:
                step(g, g + 1)
            step(NG - 1, None)

            def maxima(nxt, p):
                dve.wait_ge(S["t_sn"], 2 * nxt + p + 1)
                if p == 0:
                    wait(dve, "t_nm", nxt)
                V.tensor_reduce(nm[:, 2 * NSET * p:2 * NSET * (p + 1)], banks[:, 0:2, :].rearrange(
                    "p k (s m) -> p (k s) m", m=P), AX.X, ALU.max, negate=True).then_inc(S["t_max"], 1)

            def max_parts(nxt):
                dve.wait_ge(S["t_max"], 2 * nxt + 2)
                wait(dve, "t_mT", nxt)
                nm3 = nm[:, :].rearrange("p (j s) -> p j s", s=NSET)
                V.tensor_copy(NM[:, :, 0:NSET], nm3).then_inc(S["t_nhi"], 1)
                dve.wait_ge(S["t_nhi"], nxt + 1)
                V.tensor_tensor(NM[:, :, NSET:2 * NSET], nm3, NM[:, :, 0:NSET], ALU.subtract).then_inc(S["t_nm"], 1)

            def max_copy(nxt):
                dve.wait_ge(S["t_mT"], nxt + 1)
                wait(dve, "t_st", 2 * nxt)
                V.tensor_copy(mT[:, :], bank(7).bitcast(BF16)[:, 0:P]).then_inc(S["t_mTc"], 1)

            def attend(prev, b, early_=False):
                dve.wait_ge(S["t_pv"], 2 * prev + 2)
                wait(dve, "t_o", prev)
                V.reciprocal(osum[:, :], bank(4 + b % 2)[:, P:2 * P]).then_inc(S["t_rec"], 1)
                dve.wait_ge(S["t_rec"], prev + 1)
                wait(dve, "t_wo", prev)
                V.tensor_tensor(oT[:, :], bank(4 + b % 2)[:, 0:P], osum[:, :], ALU.mult).then_inc(S["t_o"], 1)

            def residual(prev, g, b):
                dve.wait_ge(S["t_wo"], prev + 1)
                V.tensor_tensor(seq(X, g, b), bank(6)[:, 0:P], seq(X, g, b), ALU.add).then_inc(S["t_x2"], 1)
                dve.wait_ge(S["t_x2"], prev + 1)
                stat(X, g, b, S["u_stat"])

            def cross(g):
                for b in range(GB):
                    cur = GB * g + b
                    more = not (last(g) and b == GB - 1)
                    begun = not (first(g) and b == 0)
                    if more:
                        maxima(cur + 1, 0)
                    if begun:
                        attend(cur - 1, b - 1)
                    if more:
                        maxima(cur + 1, 1)
                        max_parts(cur + 1)
                    if begun:
                        residual(cur - 1, g, b - 1)
                    if more:
                        max_copy(cur + 1)

            dve.wait_ge(S["l_cb"], NG)
            maxima(0, 0)
            maxima(0, 1)
            max_parts(0)
            max_copy(0)
            groups(dve, cross)
            attend(B - 1, B - 1)
            residual(B - 1, NG - 1, GB - 1)

            dve.wait_ge(S["u_stat"], B)
            moments(0, B, S["u_m1"], S["u_m2"], S["u_var"], 3, 2)
            dve.wait_ge(S["u_rstd"], 1)
            with dve.Fori(0, NG) as g:
                for b in range(GB):
                    normalise(seq(X3, g, b), seq(X, g, b), g, b).then_inc(S["u_x3"], 1)
                dve.wait_ge(S["u_x3"], GB * g + GB)
                V.tensor_reduce(mxs[:, 0, bass.ds(g, 1)], grp(X3, g), AX.X, ALU.max,
                                apply_absolute_value=True).then_inc(S["u_mx"], 1)

            n_scale = [0]

            def scales(k0, k1, unit_of):
                n_scale[0] += 1
                n, r = n_scale[0], slice(k0, k1)
                V.tensor_reduce(mx1[:, r], mxs[:, r, :], AX.X, ALU.max).then_inc(S["g_mx"], 1)
                unit_of().then_inc(S["g_unit"], 1)
                dve.wait_ge(S["g_unit"], n)
                dve.wait_ge(S["g_all"], n)
                V.scalar_tensor_tensor(out=sc0[:, r], in0=mxa[:, r], scalar=1.0 / AQ, in1=unit[:, r],
                                       op0=ALU.mult, op1=ALU.mult).then_inc(S["g_s0"], 1)
                dve.wait_ge(S["g_s0"], n)
                V.tensor_scalar(scale[:, r], sc0[:, r], 1e-12, None, ALU.max).then_inc(S["g_s"], 1)
                dve.wait_ge(S["g_s"], n)
                V.reciprocal(recip[:, r], scale[:, r]).then_inc(S["g_r"], 1)
                dve.wait_ge(S["g_r"], n)
                V.tensor_tensor(lev[:, r], recip[:, r], unit[:, r], ALU.mult).then_inc(S["g_lev"], 1)
                dve.wait_ge(S["g_lev"], n)

            dve.wait_ge(S["u_mx"], NG)
            scales(0, 1, lambda: V.memset(unit[:, 0:1], 1.0))

            def levels(g):
                if not first(g):
                    wait(dve, "a_n3", g)
                V.tensor_scalar(n3m[:, :], grp(X3, g), lev[:, 0:1], MAGIC, ALU.mult, ALU.add).then_inc(S["a_rnd"], 1)
                dve.wait_ge(S["a_rnd"], g + 1)
                if not first(g):
                    wait(dve, "a_nT", g)
                V.tensor_scalar(n3[:, :], n3m[:, :], -MAGIC, None, ALU.add).then_inc(S["a_n3"], 1)

            def largest_ug(g):
                for k, t in ((1, U), (2, G)):
                    dve.wait_ge(S["a_uc"], 6 * g + 3 * k)
                    V.tensor_reduce(mxs[:, k, bass.ds(g, 1)], grp(t, g, FW), AX.X, ALU.max,
                                    apply_absolute_value=True).then_inc(S["a_mx"], 1)

            levels(0)
            with dve.Fori(0, NG - 1) as g:
                levels(g + 1)
                largest_ug(g)
            largest_ug(NG - 1)
            dve.wait_ge(S["a_mx"], 2 * NG)
            scales(1, 3, lambda: V.tensor_copy(unit[:, 1:3], bc(scale[:, 0:1], [P, 2])))

            def gate(i, u):
                g = 2 * i + u
                dve.wait_ge(S["b_sig"], g + 1)
                wait(dve, "b_t", g)
                V.tensor_scalar(sq[:, :], sig[:, u], 65536.0, 65535.0, ALU.mult, ALU.min).then_inc(S["b_sq"], 1)
                dve.wait_ge(S["b_sq"], g + 1)
                V.tensor_tensor(grp(G, g, FW), ng[:, u], sq[:, :], ALU.mult).then_inc(S["b_t"], 1)
                dve.wait_ge(S["b_t"], g + 1)
                V.tensor_reduce(mxs[:, 3, bass.ds(g, 1)], grp(G, g, FW), AX.X, ALU.max,
                                apply_absolute_value=True).then_inc(S["b_mx"], 1)

            gate(0, 0)
            gate(0, 1)
            with dve.Fori(1, NG // 2) as i:
                gate(i, 0)
                gate(i, 1)
            dve.wait_ge(S["b_mx"], NG)
            scales(3, 4, lambda: V.tensor_scalar(unit[:, 3:4], scale[:, 2:3], 1.0 / 65536.0, None, ALU.mult))

            def product(i, u):
                g = 2 * i + u
                dve.wait_ge(S["c_tn"], g + 1)
                dve.wait_ge(S["b_un"], g + 1)
                V.tensor_tensor(grp(G, g, FW), tn[:, u], grp(UN, g, FW), ALU.mult).then_inc(S["c_o"], 1)
                dve.wait_ge(S["c_o"], g + 1)
                V.tensor_reduce(mxs[:, 4, bass.ds(g, 1)], grp(G, g, FW), AX.X, ALU.max,
                                apply_absolute_value=True).then_inc(S["c_mx"], 1)

            with dve.Fori(0, NG // 2) as i:
                product(i, 0)
                product(i, 1)
            dve.wait_ge(S["c_mx"], NG)
            scales(4, 5, lambda: V.tensor_tensor(unit[:, 4:5], scale[:, 3:4], scale[:, 1:2], ALU.mult))

            def product_levels(i, u):
                g = 2 * i + u
                V.tensor_scalar(grp(G, g, FW), grp(G, g, FW), lev[:, 4:5], MAGIC, ALU.mult, ALU.add).then_inc(S["d_rnd"], 1)
                dve.wait_ge(S["d_rnd"], g + 1)
                wait(dve, "d_y", g - 1)
                V.tensor_scalar(on[:, u], grp(G, g, FW), -MAGIC, None, ALU.add).then_inc(S["d_on"], 1)

            def result(i, u):
                g = 2 * i + u
                dve.wait_ge(S["d_y"], g + 1)
                wait(dve, "d_st%d" % u, 16 * i)
                V.scalar_tensor_tensor(out=y[:, u], in0=bank(u), scalar=scale[:, 4:5], in1=grp(X, g),
                                       op0=ALU.mult, op1=ALU.add).then_inc(S["d_yc"], 1)

            def turn(i):
                product_levels(i, 0)
                if not (isinstance(i, int) and i == 0):
                    result(i - 1, 1)
                product_levels(i, 1)
                result(i, 0)

            turn(0)
            turn(1)
            with dve.Fori(2, NG // 2) as i:
                turn(i)
            result(NG // 2 - 1, 1)


_INS = ["x", "ctx_1024", "mask_Bx1xS2_ik0", "L0_attn_W_qkv", "L0_xattn_Wq", "L0_xattn_bq", "L0_xattn_Wk",
        "L0_xattn_bk", "L0_xattn_Wv", "L0_xattn_bv", "L0_xattn_Wo", "L0_xattn_bo", "L0_ffn_w_gate",
        "L0_ffn_w_up", "L0_ffn_w_down"]
_OUTS = [((32, 128, 128), "float32")]


def kernel(**inputs):
    import numpy as _np
    import concourse.bacc as _bacc
    from concourse import mybir as _mybir
    from concourse.bass_utils import run_bass_kernel_spmd as _run

    nc = _bacc.Bacc("TRN2", target_bir_lowering=False, num_devices=1)
    arrays, args = {}, []
    for name in _INS:
        a = _np.ascontiguousarray(inputs[name])
        arrays[f"in_{name}_dram"] = a
        args.append(nc.dram_tensor(f"in_{name}_dram", a.shape, _mybir.dt.from_np(a.dtype), kind="ExternalInput").ap())
    for i, (shape, dtype) in enumerate(_OUTS):
        dt = _mybir.dt.from_np(_np.dtype(dtype))
        args.append(nc.dram_tensor(f"out_{i}_dram", shape, dt, kind="ExternalOutput").ap())
    decoder(nc, *args)
    r = _run(nc, [arrays], core_ids=[0])
    got = tuple(r.results[0][f"out_{i}_dram"] for i in range(len(_OUTS)))
    return got[0]
```

```python
from contextlib import ExitStack

import concourse.bass as bass
from concourse import mybir

ALU = mybir.AluOpType
ACT = mybir.ActivationFunctionType
F32 = mybir.dt.float32
F16 = mybir.dt.float16
BF16 = mybir.dt.bfloat16
I32 = mybir.dt.int32
I16 = mybir.dt.int16
U16 = mybir.dt.uint16
AX = mybir.AxisListType
RMAX = bass.bass_isa.ReduceOp.max

P = 128
B = 32
GB = 4
NG = B // GB
GT = GB * P
H = 16
DK = P // H
JT = 4
NSET = H // JT
RT = P // JT
CT = 4
VW = 16
FC = 3
QB = 32
EPS = 1e-5
MAGIC = 12582912.0
NEG = -1.0e9
CAUSAL = -1.0e30
AQ = 32767.0


def bc(ap, shape):
    return ap.broadcast_to(shape)


def decoder(nc, x, ctx_in, mask, Wqkv, Wq, bq, Wk, bk, Wv, bv, Wo, bo, w_gate, w_up, w_down, out):
    with ExitStack() as ctx:
        def sb(name, shape, dt=F32, where=ctx):
            return where.enter_context(nc.sbuf_tensor(name, shape, dt))

        def sem(name):
            return ctx.enter_context(nc.semaphore(name))

        X = sb("X", [P, B * P])
        ident = sb("ident", [P, P])
        identb = sb("identb", [P, P], BF16)
        zero_col = sb("zero_col", [P, 1])
        gateT = sb("gateT", [P, FC * P])
        upT = sb("upT", [P, FC * P])
        downT = sb("downT", [P, FC * P])
        stats = sb("stats", [P, 6 * B])
        mdif = sb("mdif", [P, B])
        msum = sb("msum", [P, B])
        mdq = sb("mdq", [P, B])
        sqs = sb("sqs", [P, B])
        mean = sb("mean", [P, B])
        vare = sb("vare", [P, B])
        rstd = sb("rstd", [P, B])
        mhalf = sb("mhalf", [P, B])
        X3 = sb("X3", [P, B * P])

        early = ExitStack()
        WS = sb("WS", [P, 3 * P], where=early)
        WX = sb("WX", [P, 4, P], where=early)
        WF = sb("WF", [P, 3, FC * P], where=early)
        WR = sb("WR", [P, 3 * FC * P], where=early)
        blkmax = sb("blkmax", [P, 36], where=early)
        blkscale = sb("blkscale", [P, 36], where=early)
        blkrecip = sb("blkrecip", [P, 36], where=early)
        WST = sb("WST", [P, 2 * P], where=early)
        A = sb("A", [P, P], where=early)
        WXT = sb("WXT", [P, 4, P], where=early)
        bcol = sb("bcol", [P, 3], where=early)
        borow = sb("borow", [1, P], where=early)
        bvrep = sb("bvrep", [P, P], where=early)
        cbias = sb("cbias", [P, P], where=early)
        ones = sb("ones", [P, P], where=early)
        causal = sb("causal", [P, P], where=early)
        M32 = sb("M32", [B, P], I32, where=early)
        MV = sb("MV", [B, P], where=early)
        nvalid = sb("nvalid", [B, 1], where=early)
        MR = sb("MR", [B, P], where=early)
        vmask = sb("vmask", [P, B], where=early)
        anyv = sb("anyv", [P, B], where=early)
        cnt1 = sb("cnt1", [P, B], where=early)
        cntr = sb("cntr", [P, B], where=early)
        vn = sb("vn", [P, B], where=early)
        bmask = sb("bmask", [P, B], where=early)
        mcol = sb("mcol", [P, 2, 2], where=early)
        sel16 = sb("sel16", [P, H], where=early)
        inj = sb("inj", [P, H, P], BF16, where=early)
        ctxg = sb("ctxg", [P, GT], where=early)
        mrow = sb("mrow", [P, GT], where=early)
        pick = sb("pick", [P, GT], where=early)
        pickd = sb("pickd", [P, GT], where=early)
        h = sb("h", [P, GT], where=early)
        hT = sb("hT", [P, GT], where=early)
        aT = sb("aT", [P, GT], where=early)
        v1 = sb("v1", [P, GT], where=early)
        sm = sb("sm", [P, GT], where=early)
        nmax = sb("nmax", [P, GB], where=early)
        pexp = sb("pexp", [P, GT], where=early)
        psum1 = sb("psum1", [P, GB], where=early)
        pinv = sb("pinv", [P, GB], where=early)
        pT = sb("pT", [P, GT], where=early)
        h2 = sb("h2", [P, GT], where=early)
        h2T = sb("h2T", [P, GT], where=early)
        cT = sb("cT", [P, GT], where=early)
        qhi = sb("qhi", [P, GT], F16, where=early)
        qlo = sb("qlo", [P, GT], F16, where=early)
        khi = sb("khi", [P, GT], F16, where=early)
        klo = sb("klo", [P, GT], F16, where=early)
        V2 = sb("V2", [P, B * P], where=early)
        VP = sb("VP", [P, 2, H, 2 * VW], where=early)
        qblk = sb("qblk", [P, 4, NSET, JT, P], F16, where=early)
        kd = sb("kd", [P, 4, NSET, P], F16, where=early)
        PT = sb("PT", [P, NSET, GT], where=early)
        nm = sb("nm", [P, 2, H], where=early)
        NM = sb("NM", [P, P], BF16, where=early)
        mT = sb("mT", [P, P], BF16, where=early)
        orec = sb("orec", [P, H], where=early)
        oun = sb("oun", [P, 2 * P], where=early)
        on_ = sb("on_", [P, P], where=early)
        oT = sb("oT", [P, P], where=early)
        early.close()

        late = ctx.enter_context(ExitStack())
        FW = FC * GT
        U = sb("U", [P, NG * FW], where=late)
        G = sb("G", [P, NG * FW], where=late)
        n3 = sb("n3", [P, GT], where=late)
        n3m = sb("n3m", [P, GT], where=late)
        n3T = sb("n3T", [P, GT], where=late)
        UN = sb("UN", [P, NG * FW], I16, where=late)
        ng = sb("ng", [P, 2, FW], I16, where=late)
        sig = sb("sig", [P, 2, FW], where=late)
        sq = sb("sq", [P, FW], U16, where=late)
        tn = sb("tn", [P, 2, FW], I16, where=late)
        on = sig
        y = sb("y", [P, 2, GT], where=late)
        mxs = sb("mxs", [P, 5, NG], where=late)
        mx1 = sb("mx1", [P, 5], where=late)
        mxa = sb("mxa", [P, 5], where=late)
        unit = sb("unit", [P, 5], where=late)
        sc0 = sb("sc0", [P, 5], where=late)
        scale = sb("scale", [P, 5], where=late)
        recip = sb("recip", [P, 5], where=late)
        lev = sb("lev", [P, 5], where=late)

        def dram(name, shape, dt):
            return nc.dram_tensor(name, shape, dt, kind="Internal").ap()

        q_dram = dram("q_dram", [B, JT, 4, RT * P], F16)
        k_dram = dram("k_dram", [B, 4, P * P], F16)
        m_dram = dram("m_dram", [B, P], F32)

        banks = ctx.enter_context(nc.psum_tensor("banks", [P, 8, GT], F32))

        def bank(n, k=1):
            return banks[:, n:n + k, :].rearrange("p k t -> p (k t)")

        names = """ld_w ld_x ld_ctx ld_m ld_wf
            c_set c_vp c_id c_causal c_wz c_sel c_inj c_bcol c_bv
            w_t1 w_t1c w_a w_ac w_t2 w_t2c w_cb w_cbc
            m_val m_n m_r m_t m_tc m_cnt m_any m_b m_c1 m_cr m_vn m_st
            f_max f_sc f_rc f_mul f_rnd f_sub f_clip f_deq f_t f_tc
            s_stat s_m1 s_m2 s_var s_rstd s_h s_hT s_hTc s_a s_ac s_v s_vc s_s s_sm s_nm s_exp s_pT s_pTc s_pv s_inv s_x1
            l_stat l_m1 l_m2 l_var l_rstd l_h l_hT l_hTc ld_mr l_pd l_pe l_pick l_cT l_cTc l_k l_khi l_klo l_q l_qhi l_qlo l_v l_vc l_cb l_qst l_kst
            t_ld0 t_ld1 t_ld2 t_ld3 t_sn t_max t_nhi t_nm t_mT t_mTc t_st t_exp t_pv t_rec t_ou t_tr t_o t_oT t_oTc t_wo t_x2 t_mk t_vp
            u_stat u_m1 u_m2 u_var u_rstd u_x3 u_mx
            g_mx g_all g_unit g_s0 g_s g_r g_lev
            a_rnd a_n3 a_nT a_nTc a_u a_uc a_mx
            b_ng b_sig b_sq b_t b_mx b_un c_tn c_o c_mx
            d_rnd d_on d_y d_yc d_st0 d_st1""".split()
        S = {n: sem(n) for n in names}

        block = ctx.enter_context(nc.Block())
        xs = x.rearrange("b s d -> s b d")
        cs = ctx_in.rearrange("b s d -> s b d")
        os = out.rearrange("b s d -> s b d")
        X4 = X[:, :].rearrange("p (b d) -> p b d", d=P)

        def groups(eng, step):
            step(0)
            with eng.Fori(1, NG - 1) as g:
                step(g)
            step(NG - 1)

        def wait(eng, name, value):
            if not (isinstance(value, int) and value <= 0):
                eng.wait_ge(S[name], value)

        def first(g):
            return isinstance(g, int) and g == 0

        def last(g):
            return isinstance(g, int) and g == NG - 1

        def seq(t, g, b):
            return t[:, bass.ds(g * GT + b * P, P)]

        def grp(t, g, w=GT):
            return t[:, bass.ds(g * w, w)]

        @block.sync
        def _(sp):
            def load_context(g):
                sp.dma_start(ctxg[:, :].rearrange("p (b d) -> p b d", d=P),
                             cs[:, bass.ds(g * GB, GB), :]).then_inc(S["ld_ctx"], 16)

            sp.dma_start(WS[:, :], Wqkv).then_inc(S["ld_w"], 16)
            for n, w in enumerate((Wq, Wk, Wv, Wo)):
                sp.dma_start(WX[:, n, :], w).then_inc(S["ld_w"], 16)
            for n, b_ in enumerate((bq, bk)):
                sp.dma_start(bcol[:, n:n + 1], b_.rearrange("(s j e o) -> j e s o", s=NSET, j=JT, o=1),
                             allow_slow_non_contiguous=True).then_inc(S["ld_w"], 16)
            sp.dma_start(bcol[:, 2:3], bv.rearrange("(p o) -> p o", o=1)).then_inc(S["ld_w"], 16)
            sp.dma_start(borow[:, :], bo.rearrange("(o d) -> o d", o=1)).then_inc(S["ld_w"], 16)
            sp.dma_start(M32[:, :], mask.rearrange("b o s -> (b o) s")).then_inc(S["ld_m"], 16)
            for q in range(4):
                r = slice(q * B // 4, (q + 1) * B // 4)
                sp.dma_start(X4[:, r, :], xs[:, r, :]).then_inc(S["ld_x"], 16)
            load_context(0)
            for n, w in enumerate((w_gate, w_up)):
                sp.dma_start(WF[:, n, :].rearrange("p (c d) -> p c d", c=FC),
                             w.rearrange("(c p) d -> p c d", c=FC)).then_inc(S["ld_wf"], 16)
            sp.dma_start(WF[:, 2, :], w_down).then_inc(S["ld_wf"], 16)
            sp.wait_ge(S["m_r"], 1)
            sp.dma_start(m_dram, MR[:, :]).then_inc(S["m_st"], 16)
            sp.wait_ge(S["m_st"], 16)
            flat = m_dram.rearrange("b s -> (b s)")

            def load_replaced(g):
                sp.dma_start(mrow[:, :], flat[bass.ds(g * GT, GT)].partition_broadcast(P)).then_inc(S["ld_mr"], 16)

            load_replaced(0)

            def store(g):
                sp.wait_ge(S["l_klo"], g + 1)
                here = bass.ds(g * GB, GB)
                for c in range(4):
                    rows = k_dram[here, c].rearrange("b (r t) -> r b t", t=P)
                    sp.dma_start(rows, (khi, klo)[c % 2][:, :].rearrange("r (b t) -> r b t", b=GB)).then_inc(S["l_kst"], 16)
                sp.wait_ge(S["l_qlo"], g + 1)
                for c in range(4):
                    for j in range(JT):
                        rows = q_dram[here, j, c].rearrange("b (r t) -> r b t", t=P)
                        sp.dma_start(rows, (qhi, qlo)[c // 2][j * RT:j * RT + RT, :].rearrange("r (b t) -> r b t", b=GB)
                                     ).then_inc(S["l_qst"], 16)

            def store_and_load(g):
                sp.wait_ge(S["l_cT"], g + 1)
                load_context(g + 1)
                load_replaced(g + 1)
                store(g)

            with sp.Fori(0, NG - 1) as g:
                store_and_load(g)
            store(NG - 1)

            sp.wait_ge(S["l_kst"], 64 * NG)
            sp.wait_ge(S["l_qst"], 256 * NG)

            sp.wait_ge(S["c_set"], 4)
            sp.wait_ge(S["c_wz"], 3)

            def fill(b, n):
                for j in range(JT):
                    r = slice(RT * j, RT * j + RT)
                    sp.dma_start(qblk[r, b, :, j, :], q_dram[n, j].rearrange("c (e s t) -> (c e) s t", e=DK, s=NSET)
                                 ).then_inc(S["t_ld%d" % b], 16)
                    sp.dma_start(kd[r, b].rearrange("p s t -> p (s t)"),
                                 k_dram[n].rearrange("c (j e x) -> j c e x", j=JT, e=DK)[j]).then_inc(S["t_ld%d" % b], 16)

            for b in range(GB):
                fill(b, b)
            with sp.Fori(1, NG) as g:
                for b in range(GB):
                    sp.wait_ge(S["t_st"], NSET * (GB * (g - 1) + b) + NSET)
                    fill(b, GB * g + b)

            with sp.Fori(0, NG // 2) as i:
                for u in range(2):
                    sp.wait_ge(S["d_yc"], 2 * i + u + 1)
                    sp.dma_start(os[:, bass.ds(i * 2 * GB + u * GB, GB), :],
                                 y[:, u].rearrange("p (b d) -> p b d", d=P)).then_inc(S["d_st%d" % u], 16)
            sp.wait_ge(S["d_st0"], 16 * NG // 2)
            sp.wait_ge(S["d_st1"], 16 * NG // 2)

        @block.gpsimd
        def _(pool):
            nc.gpsimd.memset(ident[:, :], 0.0).then_inc(S["c_set"], 1)
            nc.gpsimd.memset(causal[:, :], 0.0).then_inc(S["c_set"], 1)
            nc.gpsimd.memset(mhalf[:, :], -0.5).then_inc(S["c_set"], 1)
            pool.wait_ge(S["c_set"], 3)
            nc.gpsimd.affine_select(out=ident[:, :], in_=ident[:, :], compare_op=ALU.not_equal, fill=1.0,
                                    base=0, pattern=[[-1, P]], channel_multiplier=1).then_inc(S["c_id"], 1)
            nc.gpsimd.affine_select(out=causal[:, :], in_=causal[:, :], compare_op=ALU.is_ge, fill=CAUSAL,
                                    base=0, pattern=[[-1, P]], channel_multiplier=1).then_inc(S["c_causal"], 1)
            nc.gpsimd.memset(qblk[:, 0:2], 0.0).then_inc(S["c_set"], 1)
            pool.wait_ge(S["s_var"], 1)
            nc.gpsimd.tensor_tensor(rstd[:, :], vare[:, :], mhalf[:, :], ALU.pow).then_inc(S["s_rstd"], 1)

            pool.wait_ge(S["f_rc"], 1)
            W3 = WF[:, :, :].rearrange("p m (k e) -> p (m k) e", e=QB)
            R3 = WR[:, :].rearrange("p (k e) -> p k e", e=QB)
            wide = [P, 3 * FC * P // QB, QB]
            WR1 = WR[:, :]
            nc.gpsimd.tensor_tensor(R3, W3, bc(blkrecip[:, :].unsqueeze(2), wide), ALU.mult).then_inc(S["f_mul"], 1)
            pool.wait_ge(S["f_mul"], 1)
            nc.gpsimd.tensor_scalar(WR1, WR1, MAGIC, None, ALU.add).then_inc(S["f_rnd"], 1)
            pool.wait_ge(S["f_rnd"], 1)
            nc.gpsimd.tensor_scalar(WR1, WR1, -MAGIC, None, ALU.add).then_inc(S["f_sub"], 1)
            pool.wait_ge(S["f_sub"], 1)
            nc.gpsimd.tensor_scalar(WR1, WR1, 7.0, -8.0, ALU.min, ALU.max).then_inc(S["f_clip"], 1)
            pool.wait_ge(S["f_clip"], 1)
            nc.gpsimd.tensor_tensor(R3, R3, bc(blkscale[:, :].unsqueeze(2), wide), ALU.mult).then_inc(S["f_deq"], 1)

            def picker(g):
                four = [P, GB, P]
                idb = bc(ident[:, :].unsqueeze(1), four)
                pickd4, pick4 = (t[:, :].rearrange("p (b k) -> p b k", b=GB) for t in (pickd, pick))
                wait(pool, "l_pick", g)
                nc.gpsimd.tensor_tensor(pickd4, bc(vn[:, bass.ds(g * GB, GB)].unsqueeze(2), four), idb,
                                        ALU.subtract).then_inc(S["l_pd"], 1)
                pool.wait_ge(S["l_pd"], g + 1)
                pool.wait_ge(S["ld_mr"], 16 * g + 16)
                nc.gpsimd.tensor_tensor(pickd[:, :], pickd[:, :], mrow[:, :], ALU.mult).then_inc(S["l_pe"], 1)
                pool.wait_ge(S["l_pe"], g + 1)
                wait(pool, "l_cT", g)
                nc.gpsimd.tensor_tensor(pick4, pickd4, idb, ALU.add).then_inc(S["l_pick"], 1)

            pool.wait_ge(S["m_vn"], 1)
            picker(0)

            def second(g):
                pool.wait_ge(S["l_var"], g + 1)
                nc.gpsimd.tensor_tensor(rstd[:, bass.ds(g * GB, GB)], vare[:, bass.ds(g * GB, GB)],
                                        mhalf[:, 0:GB], ALU.pow).then_inc(S["l_rstd"], 1)
                pool.wait_ge(S["l_h"], GB * g + GB)
                pool.wait_ge(S["w_cbc"], 1)
                xg = grp(X, g).rearrange("p (b d) -> p b d", d=P)
                nc.gpsimd.tensor_tensor(xg, xg, bc(cbias[:, :].unsqueeze(1), [P, GB, P]), ALU.add).then_inc(S["l_cb"], 1)

            with pool.Fori(0, NG - 1) as g:
                second(g)
                picker(g + 1)
            second(NG - 1)

            pool.wait_ge(S["l_vc"], NG)
            pool.wait_ge(S["c_vp"], 1)

            def mask_columns(g):
                for b in range(GB):
                    if not (first(g) and b < 2):
                        pool.wait_ge(S["t_pv"], NSET * (GB * g + b) - NSET)
                    nc.gpsimd.tensor_copy(mcol[:, b % 2, 0:1], vmask[:, bass.ds(GB * g + b, 1)]).then_inc(S["t_mk"], 1)
                    nc.gpsimd.tensor_copy(mcol[:, b % 2, 1:2], bmask[:, bass.ds(GB * g + b, 1)]).then_inc(S["t_mk"], 1)
                    src = seq(V2, g, b).rearrange("p (a k j e) -> p a k j e", a=2, k=2, j=JT)
                    dst = VP[:, b % 2].rearrange("p (a k j) c -> p a k j c", a=2, k=2)
                    for k in range(2):
                        nc.gpsimd.tensor_copy(dst[:, :, k, :, VW * k:VW * k + DK], src[:, :, k]).then_inc(S["t_vp"], 1)

            groups(pool, mask_columns)

            pool.wait_ge(S["u_var"], 1)
            nc.gpsimd.tensor_tensor(rstd[:, :], vare[:, :], mhalf[:, :], ALU.pow).then_inc(S["u_rstd"], 1)
            for n, (k0, k1) in enumerate(((0, 1), (1, 3), (3, 4), (4, 5))):
                pool.wait_ge(S["g_mx"], n + 1)
                nc.gpsimd.partition_all_reduce(mxa[:, k0:k1], mx1[:, k0:k1], P, RMAX).then_inc(S["g_all"], 1)

        @block.tensor
        def _(pe):
            pe.wait_ge(S["c_id"], 1)
            pe.wait_ge(S["ld_w"], 16 * 9)
            pe.transpose(bank(0)[:, 0:P], WS[:, 0:P], ident[:, :])
            pe.transpose(bank(0)[:, P:2 * P], WS[:, P:2 * P], ident[:, :]).then_inc(S["w_t1"], 1)
            for n in range(4):
                m = pe.transpose(bank(2)[:, n * P:(n + 1) * P], WX[:, n, :], ident[:, :])
            m.then_inc(S["w_t2"], 1)
            pe.wait_ge(S["w_t1c"], 1)
            pe.matmul(bank(1)[:, 0:P], WST[:, 0:P], WST[:, P:2 * P], start=True, stop=True).then_inc(S["w_a"], 1)
            pe.wait_ge(S["w_t2c"], 3)
            pe.wait_ge(S["c_bv"], 1)
            pe.wait_ge(S["c_wz"], 1)
            pe.matmul(bank(3)[:, 0:P], bvrep[:, :], WXT[:, 3, :], start=True, stop=False)
            pe.matmul(bank(3)[:, 0:P], ones[0:1, :], borow[:, :], start=False, stop=True).then_inc(S["w_cb"], 1)
            pe.wait_ge(S["m_val"], 1)
            pe.transpose(bank(4)[:, 0:B], MV[:, :], ident[0:B, 0:B]).then_inc(S["m_t"], 1)
            pe.wait_ge(S["m_tc"], 1)
            pe.matmul(bank(5)[:, 0:B], ones[:, :], vmask[:, :], start=True, stop=True).then_inc(S["m_cnt"], 1)
            pe.wait_ge(S["w_ac"], 1)
            pe.wait_ge(S["w_cbc"], 1)
            pe.wait_ge(S["m_b"], 1)

            def transposes(n, src):
                for b in range(GB):
                    m = pe.transpose(bank(n)[:, b * P:(b + 1) * P], src(b), ident[:, :])
                return m

            def step(cur, nxt):
                if cur is not None:
                    pe.wait_ge(S["s_exp"], GB * cur + GB)
                    wait(pe, "l_hTc", cur)
                    transposes(5, lambda b: pexp[:, b * P:(b + 1) * P]).then_inc(S["s_pT"], 1)
                if nxt is not None:
                    pe.wait_ge(S["s_h"], GB * nxt + GB)
                    wait(pe, "s_hTc", nxt)
                    transposes(0, lambda b: h[:, b * P:(b + 1) * P]).then_inc(S["s_hT"], 1)
                if cur is not None:
                    pe.wait_ge(S["ld_ctx"], 16 * cur + 16)
                    wait(pe, "l_vc", cur)
                    pe.wait_ge(S["l_pick"], cur + 1)
                    for b in range(GB):
                        r = slice(b * P, (b + 1) * P)
                        m = pe.matmul(bank(1)[:, r], ctxg[:, r], pick[:, r], start=True, stop=True)
                    m.then_inc(S["l_cT"], 1)
                    pe.wait_ge(S["s_pTc"], cur + 1)
                    pe.wait_ge(S["s_vc"], cur + 1)
                    wait(pe, "l_qlo", cur)
                    for b in range(GB):
                        r = slice(b * P, (b + 1) * P)
                        m = pe.matmul(bank(6)[:, r], pT[:, r], v1[:, r], start=True, stop=True)
                    m.then_inc(S["s_pv"], 1)
                if nxt is not None:
                    pe.wait_ge(S["s_hTc"], nxt + 1)
                    wait(pe, "s_ac", nxt)
                    pe.matmul(bank(2), A[:, :], hT[:, :], start=True, stop=True).then_inc(S["s_a"], 1)
                    wait(pe, "s_vc", nxt)
                    for b in range(GB):
                        r = slice(b * P, (b + 1) * P)
                        m = pe.matmul(bank(3)[:, r], hT[:, r], WS[:, 2 * P:3 * P], start=True, stop=True)
                    m.then_inc(S["s_v"], 1)
                if cur is not None:
                    pe.wait_ge(S["l_cTc"], cur + 1)
                    wait(pe, "l_klo", cur)
                    pe.matmul(bank(7), WXT[:, 1, :], cT[:, :], start=True, stop=True).then_inc(S["l_k"], 1)
                if nxt is not None:
                    pe.wait_ge(S["s_ac"], nxt + 1)
                    wait(pe, "s_sm", nxt)
                    for b in range(GB):
                        r = slice(b * P, (b + 1) * P)
                        m = pe.matmul(bank(4)[:, r], aT[:, r], hT[:, r], start=True, stop=True)
                    m.then_inc(S["s_s"], 1)
                if cur is not None:
                    for b in range(GB):
                        r = slice(b * P, (b + 1) * P)
                        m = pe.matmul(bank(1)[:, r], cT[:, r], WXT[:, 2, :], start=True, stop=True)
                    m.then_inc(S["l_v"], 1)
                    pe.wait_ge(S["l_h"], GB * cur + GB)
                    transposes(5, lambda b: h2[:, b * P:(b + 1) * P]).then_inc(S["l_hT"], 1)
                    pe.wait_ge(S["l_hTc"], cur + 1)
                    pe.wait_ge(S["s_x1"], GB * cur + GB)
                    pe.matmul(bank(6), WXT[:, 0, :], h2T[:, :], start=True, stop=True).then_inc(S["l_q"], 1)

            step(None, 0)
            step(0, 1)
            with pe.Fori(1, NG - 1) as g:
                step(g, g + 1)
            step(NG - 1, None)

            pe.wait_ge(S["f_deq"], 1)
            pe.wait_ge(S["s_hTc"], NG)
            pe.wait_ge(S["l_vc"], NG)
            for m_ in range(3):
                for c in range(FC):
                    w = WR[:, m_ * FC * P + c * P:m_ * FC * P + (c + 1) * P]
                    m = pe.transpose(bank(m_)[:, c * P:(c + 1) * P], w, ident[:, :])
            m.then_inc(S["f_t"], 1)
            pe.wait_ge(S["f_tc"], 3)
            pe.wait_ge(S["l_qlo"], NG)
            pe.wait_ge(S["l_klo"], NG)
            pe.wait_ge(S["l_hTc"], NG)
            pe.wait_ge(S["c_inj"], 1)

            def scores_q(n, s, b):
                if not (isinstance(n, int) and NSET * n + s < 2):
                    pe.wait_ge(S["t_max"], NSET * n + s - 1)
                for j in range(JT):
                    m = pe.matmul(bank(s % 2)[:, j * P:(j + 1) * P], qblk[:, b % GB, s, j, :], kd[:, b % GB, s, :],
                                  start=True, stop=True)
                m.then_inc(S["t_sn"], 1)

            def scores_k(n, s, b):
                if not (isinstance(n, int) and NSET * n + s < 2):
                    pe.wait_ge(S["t_exp"], NSET * n + s - 1)
                pe.matmul(bank(2 + s % 2), kd[:, b % GB, s, :], qblk[:, b % GB, s, :, :].rearrange("p j t -> p (j t)"),
                          start=True, stop=False, skip_group_check=True)
                for j in range(JT):
                    m = pe.matmul(bank(2 + s % 2)[:, j * P:(j + 1) * P], inj[:, JT * s + j, :], mT[:, :],
                                  start=False, stop=(j == JT - 1), skip_group_check=True)
                m.then_inc(S["t_st"], 1)

            def pv(n, s, b):
                pe.wait_ge(S["t_exp"], NSET * n + s + 1)
                for j in range(JT):
                    m = pe.matmul(bank(4 + b % 2)[RT * j:RT * j + RT, s // 2 * P:s // 2 * P + P],
                                  VP[:, b % 2, JT * s + j, :], PT[:, s, j * P:(j + 1) * P],
                                  start=(s % 2 == 0), stop=(s % 2 == 1), skip_group_check=True,
                                  tile_position=(0, RT * j))
                m.then_inc(S["t_pv"], 1)

            def max_rows(n):
                pe.wait_ge(S["t_nm"], n + 1)
                wait(pe, "t_mTc", n)
                pe.transpose(bank(6).bitcast(BF16)[:, 0:P], NM[:, :], identb[:, :]).then_inc(S["t_mT"], 1)

            def queries(n):
                pe.wait_ge(S["t_ou"], n + 1)
                wait(pe, "t_x2", n)
                for a in range(2):
                    m = pe.transpose(bank(7)[:, (2 + a) * P:(3 + a) * P], oun[:, a * P:(a + 1) * P], ident[:, :])
                m.then_inc(S["t_tr"], 1)

            def turn(n):
                pe.wait_ge(S["t_o"], 2 * n + 2)
                pe.transpose(bank(7)[:, 0:P], on_[:, :], ident[:, :]).then_inc(S["t_oT"], 1)

            def project(n):
                pe.wait_ge(S["t_oTc"], n + 1)
                pe.matmul(bank(7)[:, P:2 * P], oT[:, :], WXT[:, 3, :], start=True, stop=True).then_inc(S["t_wo"], 1)

            def cross(g):
                for b in range(GB):
                    cur = GB * g + b
                    more = not (last(g) and b == GB - 1)
                    begun = not (first(g) and b == 0)
                    if more:
                        pe.wait_ge(S["t_ld%d" % ((b + 1) % GB)], 128 * g + (128 if b < GB - 1 else 256))
                        scores_q(cur + 1, 0, b + 1)
                        scores_q(cur + 1, 1, b + 1)
                    pe.wait_ge(S["t_mTc"], cur + 1)
                    scores_k(cur, 0, b)
                    if begun:
                        pv(cur - 1, 3, b - 1)
                    if more:
                        scores_q(cur + 1, 2, b + 1)
                    scores_k(cur, 1, b)
                    pe.wait_ge(S["t_vp"], 2 * cur + 2)
                    if not (first(g) and b < 2):
                        wait(pe, "t_ou", cur - 1)
                    pv(cur, 0, b)
                    if begun:
                        queries(cur - 1)
                    if more:
                        scores_q(cur + 1, 3, b + 1)
                    scores_k(cur, 2, b)
                    pv(cur, 1, b)
                    if begun:
                        turn(cur - 1)
                    scores_k(cur, 3, b)
                    pv(cur, 2, b)
                    if begun:
                        project(cur - 1)
                    if more:
                        max_rows(cur + 1)

            pe.wait_ge(S["c_wz"], 6)
            pe.wait_ge(S["t_ld0"], 128)
            for s in range(NSET):
                scores_q(0, s, 0)
            max_rows(0)
            groups(pe, cross)
            pv(B - 1, 3, GB - 1)
            queries(B - 1)
            turn(B - 1)
            project(B - 1)

            def up_gate(g):
                pe.wait_ge(S["a_n3"], g + 1)
                if not first(g):
                    wait(pe, "a_nTc", g)
                transposes(0, lambda b: n3[:, b * P:(b + 1) * P]).then_inc(S["a_nT"], 1)
                pe.wait_ge(S["a_nTc"], g + 1)
                for k in range(6):
                    if not first(g):
                        pe.wait_ge(S["a_uc"], 6 * g - 5 + k)
                    w = (upT, gateT)[k // FC]
                    pe.matmul(bank(2 + k), w[:, k % FC * P:k % FC * P + P], n3T[:, :],
                              start=True, stop=True).then_inc(S["a_u"], 1)

            pe.wait_ge(S["t_x2"], B)
            groups(pe, up_gate)

            def down(i, u, begun):
                g = 2 * i + u
                pe.wait_ge(S["d_on"], g + 1)
                if begun:
                    pe.wait_ge(S["d_yc"], g - 1)
                for b in range(GB):
                    for c in range(FC):
                        m = pe.matmul(bank(u)[:, b * P:(b + 1) * P], on[:, u, c * GT + b * P:c * GT + b * P + P],
                                      downT[:, c * P:(c + 1) * P], start=(c == 0), stop=(c == FC - 1))
                m.then_inc(S["d_y"], 1)

            down(0, 0, False)
            down(0, 1, False)
            with pe.Fori(1, NG // 2) as i:
                down(i, 0, True)
                down(i, 1, True)

        @block.scalar
        def _(act):
            act.preload_act_table(ACT.Exp)
            act.wait_ge(S["w_t1"], 1)
            act.activation(WST[:, :], bank(0)[:, 0:2 * P], ACT.Copy).then_inc(S["w_t1c"], 1)
            act.wait_ge(S["w_t2"], 1)
            for n, c in ((0, float(DK) ** -0.5), (1, 1.0)):
                act.activation(WXT[:, n, :].rearrange("p (j e s) -> p s j e", j=JT, s=NSET),
                               bank(2)[:, n * P:(n + 1) * P].rearrange("p (s j e) -> p s j e", j=JT, s=NSET),
                               ACT.Copy, scale=c).then_inc(S["w_t2c"], 1)
            act.activation(WXT[:, 2:4, :].rearrange("p n d -> p (n d)"), bank(2)[:, 2 * P:4 * P], ACT.Copy).then_inc(S["w_t2c"], 1)
            act.wait_ge(S["w_a"], 1)
            act.activation(A[:, :], bank(1)[:, 0:P], ACT.Copy, scale=float(P) ** -0.5).then_inc(S["w_ac"], 1)
            act.wait_ge(S["c_bcol"], 1)

            def step(cur, nxt):
                if nxt is not None:
                    act.wait_ge(S["s_hT"], nxt + 1)
                    wait(act, "s_s", nxt)
                    act.activation(hT[:, :], bank(0), ACT.Copy).then_inc(S["s_hTc"], 1)
                if cur is not None:
                    act.wait_ge(S["l_cT"], cur + 1)
                    wait(act, "l_v", cur)
                    act.activation(cT[:, :], bank(1), ACT.Copy).then_inc(S["l_cTc"], 1)
                if nxt is not None:
                    act.wait_ge(S["s_a"], nxt + 1)
                    act.activation(aT[:, :], bank(2), ACT.Copy).then_inc(S["s_ac"], 1)
                    act.wait_ge(S["s_v"], nxt + 1)
                    wait(act, "s_pv", nxt)
                    act.activation(v1[:, :], bank(3), ACT.Copy).then_inc(S["s_vc"], 1)
                if cur is not None:
                    act.wait_ge(S["l_k"], cur + 1)
                    wait(act, "l_kst", 64 * cur)
                    act.activation(khi[:, :], bank(7), ACT.Identity, bias=bcol[:, 1:2]).then_inc(S["l_khi"], 1)
                    act.wait_ge(S["l_v"], cur + 1)
                    act.activation(grp(V2, cur), bank(1), ACT.Copy).then_inc(S["l_vc"], 1)
                if nxt is not None:
                    act.wait_ge(S["s_nm"], nxt + 1)
                    wait(act, "s_pT", nxt)
                    wait(act, "s_inv", nxt)
                    for b in range(GB):
                        r = slice(b * P, (b + 1) * P)
                        act.activation(pexp[:, r], sm[:, r], ACT.Exp, bias=nmax[:, b:b + 1],
                                       accum_out=psum1[:, b:b + 1]).then_inc(S["s_exp"], 1)
                if cur is not None:
                    act.wait_ge(S["l_hT"], cur + 1)
                    wait(act, "l_q", cur)
                    act.activation(h2T[:, :], bank(5), ACT.Copy).then_inc(S["l_hTc"], 1)
                    act.wait_ge(S["l_q"], cur + 1)
                    wait(act, "l_qst", 256 * cur)
                    act.activation(qhi[:, :], bank(6), ACT.Identity, bias=bcol[:, 0:1]).then_inc(S["l_qhi"], 1)

            step(None, 0)
            step(0, 1)
            with act.Fori(1, NG - 1) as g:
                step(g, g + 1)
            step(NG - 1, None)

            act.wait_ge(S["f_t"], 1)
            for n, w in enumerate((gateT, upT, downT)):
                act.activation(w[:, :], bank(n)[:, 0:FC * P], ACT.Copy).then_inc(S["f_tc"], 1)

            def max_copy(n):
                act.wait_ge(S["t_mT"], n + 1)
                wait(act, "t_st", NSET * n)
                act.activation(mT[:, :], bank(6).bitcast(BF16)[:, 0:P], ACT.Copy).then_inc(S["t_mTc"], 1)

            def out_copy(n, b):
                act.wait_ge(S["t_pv"], NSET * n + NSET)
                wait(act, "t_tr", n)
                act.activation(oun[:, :], bank(4 + b % 2)[:, 0:2 * P], ACT.Copy).then_inc(S["t_ou"], 1)

            def turn_copy(n):
                act.wait_ge(S["t_oT"], n + 1)
                wait(act, "t_wo", n)
                act.activation(oT[:, :], bank(7)[:, 0:P], ACT.Copy).then_inc(S["t_oTc"], 1)

            def probs(g):
                for b in range(GB):
                    n = GB * g + b
                    for s in range(NSET):
                        if s == 0:
                            act.wait_ge(S["t_mk"], 2 * n + 2)
                        act.wait_ge(S["t_st"], NSET * n + s + 1)
                        if not (first(g) and b == 0):
                            act.wait_ge(S["t_pv"], NSET * n - NSET + s + 1)
                        act.activation(PT[:, s, :], bank(2 + s % 2), ACT.Exp, bias=mcol[:, b % 2, 1:2],
                                       scale=mcol[:, b % 2, 0:1]).then_inc(S["t_exp"], 1)
                        if s == 0 and not (first(g) and b == 0):
                            out_copy(n - 1, b - 1)
                        if s == 2 and not (first(g) and b == 0):
                            turn_copy(n - 1)
                    if not (last(g) and b == GB - 1):
                        max_copy(n + 1)

            max_copy(0)
            groups(act, probs)
            out_copy(B - 1, B - 1)
            turn_copy(B - 1)

            act.wait_ge(S["t_x2"], B)

            def up_gate(g):
                act.wait_ge(S["a_nT"], g + 1)
                if not first(g):
                    act.wait_ge(S["a_u"], 6 * g)
                act.activation(n3T[:, :], bank(0), ACT.Copy).then_inc(S["a_nTc"], 1)
                for k in range(6):
                    act.wait_ge(S["a_u"], 6 * g + k + 1)
                    act.activation((U, G)[k // FC][:, bass.ds(g * FW + k % FC * GT, GT)], bank(2 + k),
                                   ACT.Copy).then_inc(S["a_uc"], 1)

            groups(act, up_gate)

            act.wait_ge(S["g_lev"], 2)
            act.preload_act_table(ACT.Sigmoid)

            def gate(i, u, begun):
                g = 2 * i + u
                if begun:
                    act.wait_ge(S["b_t"], g - 1)
                act.activation(ng[:, u], grp(G, g, FW), ACT.Copy, scale=lev[:, 2:3]).then_inc(S["b_ng"], 1)
                act.activation(grp(UN, g, FW), grp(U, g, FW), ACT.Copy, scale=lev[:, 1:2]).then_inc(S["b_un"], 1)
                act.wait_ge(S["b_ng"], g + 1)
                if begun:
                    act.wait_ge(S["b_sq"], g - 1)
                act.activation(sig[:, u], ng[:, u], ACT.Sigmoid, scale=scale[:, 2:3]).then_inc(S["b_sig"], 1)

            def pairs(step):
                step(0, 0, False)
                step(0, 1, False)
                with act.Fori(1, NG // 2) as i:
                    step(i, 0, True)
                    step(i, 1, True)

            pairs(gate)

            act.wait_ge(S["g_lev"], 3)

            def gated(i, u, begun):
                g = 2 * i + u
                if begun:
                    act.wait_ge(S["c_o"], g - 1)
                act.activation(tn[:, u], grp(G, g, FW), ACT.Copy, scale=lev[:, 3:4]).then_inc(S["c_tn"], 1)

            pairs(gated)

        @block.vector
        def _(dve):
            V = nc.vector
            V.memset(ones[:, :], 1.0).then_inc(S["c_wz"], 1)
            V.memset(zero_col[:, :], 0.0).then_inc(S["c_wz"], 1)
            V.memset(qblk[:, 2:4], 0.0).then_inc(S["c_wz"], 1)
            V.memset(NM[:, :], 0.0).then_inc(S["c_wz"], 1)
            V.memset(VP[:, :, :, :], 0.0).then_inc(S["c_wz"], 1)
            dve.wait_ge(S["c_id"], 1)
            V.tensor_copy(identb[:, :], ident[:, :]).then_inc(S["c_wz"], 1)
            dve.wait_ge(S["c_wz"], 5)
            for k in range(2):
                heads = VP[:, :, :, :].rearrange("p u (a k j) c -> p k (u a) j c", a=2, k=2)[:, k]
                m = V.memset(heads[:, :, :, VW * k + DK:VW * k + DK + 1], 1.0)
            m.then_inc(S["c_vp"], 1)
            V.tensor_tensor(sel16[:, :], ident[:, 0:H], ident[:, H:2 * H], ALU.add).then_inc(S["c_sel"], 1)
            dve.wait_ge(S["c_sel"], 1)
            V.tensor_copy(inj[:, :, :], bc(sel16[:, :].unsqueeze(2), [P, H, P])).then_inc(S["c_inj"], 1)
            dve.wait_ge(S["ld_w"], 16 * 9)
            V.tensor_scalar(bcol[:, 0:1], bcol[:, 0:1], float(DK) ** -0.5, None, ALU.mult).then_inc(S["c_bcol"], 1)
            V.tensor_scalar(bvrep[:, :], ones[:, :], bcol[:, 2:3], None, ALU.mult).then_inc(S["c_bv"], 1)
            dve.wait_ge(S["ld_m"], 16)
            V.tensor_scalar(MV[:, :], M32[:, :], 0.0, None, ALU.not_equal).then_inc(S["m_val"], 1)
            dve.wait_ge(S["m_val"], 1)
            V.tensor_reduce(nvalid[:, :], MV[:, :], AX.X, ALU.max).then_inc(S["m_n"], 1)
            dve.wait_ge(S["m_n"], 1)
            V.tensor_scalar(MR[:, :], MV[:, :], 0.0, nvalid[:, 0:1], ALU.is_equal, ALU.mult).then_inc(S["m_r"], 1)
            dve.wait_ge(S["m_t"], 1)
            V.tensor_copy(vmask[:, :], bank(4)[:, 0:B]).then_inc(S["m_tc"], 1)
            dve.wait_ge(S["m_cnt"], 1)
            V.tensor_scalar(anyv[:, :], bank(5)[:, 0:B], 1.0, -NEG, ALU.min, ALU.mult).then_inc(S["m_any"], 1)
            V.tensor_scalar(cnt1[:, :], bank(5)[:, 0:B], 1.0, None, ALU.max).then_inc(S["m_c1"], 1)
            dve.wait_ge(S["m_c1"], 1)
            V.reciprocal(cntr[:, :], cnt1[:, :]).then_inc(S["m_cr"], 1)
            dve.wait_ge(S["m_cr"], 1)
            V.tensor_tensor(vn[:, :], vmask[:, :], cntr[:, :], ALU.mult).then_inc(S["m_vn"], 1)
            dve.wait_ge(S["m_any"], 1)
            V.scalar_tensor_tensor(out=bmask[:, :], in0=vmask[:, :], scalar=-1.0, in1=anyv[:, :],
                                   op0=ALU.add, op1=ALU.mult).then_inc(S["m_b"], 1)
            dve.wait_ge(S["w_cb"], 1)
            V.tensor_copy(cbias[:, :], bank(3)[:, 0:P]).then_inc(S["w_cbc"], 1)
            dve.wait_ge(S["ld_wf"], 48)
            V.tensor_reduce(blkmax[:, :], WF[:, :, :].rearrange("p m (k e) -> p (m k) e", e=QB), AX.X, ALU.max,
                            apply_absolute_value=True).then_inc(S["f_max"], 1)
            dve.wait_ge(S["f_max"], 1)
            V.tensor_scalar(blkscale[:, :], blkmax[:, :], 1.0 / 7.0, 1e-12, ALU.mult, ALU.max).then_inc(S["f_sc"], 1)
            dve.wait_ge(S["f_sc"], 1)
            V.reciprocal(blkrecip[:, :], blkscale[:, :]).then_inc(S["f_rc"], 1)

            def stat(t, g, b, s):
                V.bn_stats(stats[:, bass.ds(6 * (GB * g + b), 6)], seq(t, g, b)).then_inc(s, 1)

            even_odd = stats[:, :].rearrange("p (b f) -> p b f", f=6)

            def moments(b0, n, s_1, s_2, s_3, done1, done2):
                r, q = bass.ds(b0, n), bass.ds(b0, n)
                me, mo = even_odd[:, r, 1], even_odd[:, r, 4]
                V.tensor_tensor(mdif[:, q], me, mo, ALU.subtract).then_inc(s_1, 1)
                V.tensor_tensor(msum[:, q], me, mo, ALU.add).then_inc(s_1, 1)
                V.scalar_tensor_tensor(out=sqs[:, q], in0=even_odd[:, r, 2], scalar=P * EPS, in1=even_odd[:, r, 5],
                                       op0=ALU.add, op1=ALU.add).then_inc(s_1, 1)
                dve.wait_ge(s_1, done1)
                V.tensor_scalar(mean[:, q], msum[:, q], 0.5, None, ALU.mult).then_inc(s_2, 1)
                V.scalar_tensor_tensor(out=mdq[:, q], in0=mdif[:, q], scalar=0.25, in1=mdif[:, q],
                                       op0=ALU.mult, op1=ALU.mult).then_inc(s_2, 1)
                dve.wait_ge(s_2, done2)
                V.scalar_tensor_tensor(out=vare[:, q], in0=sqs[:, q], scalar=1.0 / P, in1=mdq[:, q],
                                       op0=ALU.mult, op1=ALU.add).then_inc(s_3, 1)

            dve.wait_ge(S["ld_x"], 64)
            with dve.Fori(0, NG) as g:
                for b in range(GB):
                    stat(X, g, b, S["s_stat"])
            dve.wait_ge(S["s_stat"], B)
            moments(0, B, S["s_m1"], S["s_m2"], S["s_var"], 3, 2)
            dve.wait_ge(S["s_m2"], 2)
            dve.wait_ge(S["s_rstd"], 1)
            dve.wait_ge(S["c_causal"], 1)

            def normalise(dst, src, g, b):
                return V.tensor_scalar(dst, src, mean[:, bass.ds(GB * g + b, 1)], rstd[:, bass.ds(GB * g + b, 1)],
                                       ALU.subtract, ALU.mult)

            def step(cur, nxt):
                if nxt is not None:
                    wait(dve, "s_hT", nxt)
                    for b in range(GB):
                        normalise(h[:, b * P:(b + 1) * P], seq(X, nxt, b), nxt, b).then_inc(S["s_h"], 1)
                if cur is not None:
                    dve.wait_ge(S["s_pT"], cur + 1)
                    wait(dve, "s_pv", cur)
                    V.tensor_copy(pT[:, :], bank(5)).then_inc(S["s_pTc"], 1)
                    wait(dve, "s_x1", GB * cur)
                    V.reciprocal(pinv[:, :], psum1[:, :]).then_inc(S["s_inv"], 1)
                    dve.wait_ge(S["s_pv"], cur + 1)
                    dve.wait_ge(S["s_inv"], cur + 1)
                    for b in range(GB):
                        V.scalar_tensor_tensor(out=seq(X, cur, b), in0=bank(6)[:, b * P:(b + 1) * P],
                                               scalar=pinv[:, b:b + 1], in1=seq(X, cur, b),
                                               op0=ALU.mult, op1=ALU.add).then_inc(S["s_x1"], 1)
                    dve.wait_ge(S["s_x1"], GB * cur + GB)
                    for b in range(GB):
                        stat(X, cur, b, S["l_stat"])
                    dve.wait_ge(S["l_stat"], GB * cur + GB)
                    moments(GB * cur, GB, S["l_m1"], S["l_m2"], S["l_var"], 3 * cur + 3, 2 * cur + 2)
                if nxt is not None:
                    dve.wait_ge(S["s_s"], nxt + 1)
                    wait(dve, "s_exp", GB * nxt)
                    V.tensor_tensor(sm[:, :].rearrange("p (b m) -> p b m", m=P),
                                    bank(4).rearrange("p (b m) -> p b m", m=P),
                                    bc(causal[:, :].unsqueeze(1), [P, GB, P]), ALU.add).then_inc(S["s_sm"], 1)
                    dve.wait_ge(S["s_sm"], nxt + 1)
                    V.tensor_reduce(nmax[:, :], sm[:, :].rearrange("p (b m) -> p b m", m=P), AX.X, ALU.max,
                                    negate=True).then_inc(S["s_nm"], 1)
                if cur is not None:
                    dve.wait_ge(S["l_khi"], cur + 1)
                    wait(dve, "l_kst", 64 * cur)
                    V.scalar_tensor_tensor(out=klo[:, :], in0=bank(7), scalar=bcol[:, 1:2], in1=khi[:, :],
                                           op0=ALU.add, op1=ALU.subtract).then_inc(S["l_klo"], 1)
                    dve.wait_ge(S["l_rstd"], cur + 1)
                    wait(dve, "l_hT", cur)
                    for b in range(GB):
                        normalise(h2[:, b * P:(b + 1) * P], seq(X, cur, b), cur, b).then_inc(S["l_h"], 1)
                    dve.wait_ge(S["l_qhi"], cur + 1)
                    wait(dve, "l_qst", 256 * cur)
                    V.scalar_tensor_tensor(out=qlo[:, :], in0=bank(6), scalar=bcol[:, 0:1], in1=qhi[:, :],
                                           op0=ALU.add, op1=ALU.subtract).then_inc(S["l_qlo"], 1)

            step(None, 0)
            step(0, 1)
            with dve.Fori(1, NG - 1) as g:
                step(g, g + 1)
            step(NG - 1, None)

            def maxima(n, s, b):
                dve.wait_ge(S["t_sn"], NSET * n + s + 1)
                if s == 0:
                    wait(dve, "t_nm", n - 1)
                V.tensor_reduce(nm[:, b % 2, JT * s:JT * s + JT], bank(s % 2).rearrange("p (j m) -> p j m", m=P),
                                AX.X, ALU.max, negate=True).then_inc(S["t_max"], 1)

            def max_parts(n, b):
                dve.wait_ge(S["t_max"], NSET * n + NSET)
                wait(dve, "t_mT", n)
                V.tensor_copy(NM[:, 0:H], nm[:, b % 2, :]).then_inc(S["t_nhi"], 1)
                dve.wait_ge(S["t_nhi"], n + 1)
                V.tensor_tensor(NM[:, H:2 * H], nm[:, b % 2, :], NM[:, 0:H], ALU.subtract).then_inc(S["t_nm"], 1)

            def attend(n):
                dve.wait_ge(S["t_tr"], n + 1)
                wait(dve, "t_o", 2 * n)
                o3 = bank(7)[:, 2 * P:4 * P].rearrange("p (h c) -> p h c", c=VW)
                V.reciprocal(orec[:, :], o3[:, :, DK]).then_inc(S["t_rec"], 1)
                dve.wait_ge(S["t_rec"], n + 1)
                wait(dve, "t_oT", n)
                for a in range(2):
                    hs = slice(a * H // 2, (a + 1) * H // 2)
                    V.tensor_tensor(on_[:, a * P // 2:(a + 1) * P // 2].rearrange("p (k j e) -> p j k e", k=2, j=JT),
                                    o3[:, hs, 0:DK].rearrange("p (j k) e -> p j k e", j=JT),
                                    bc(orec[:, hs].rearrange("p (j k) -> p j k", j=JT).unsqueeze(3),
                                       [P, JT, 2, DK]), ALU.mult).then_inc(S["t_o"], 1)

            def residual(n, g, b):
                dve.wait_ge(S["t_wo"], n + 1)
                V.tensor_tensor(seq(X, g, b), bank(7)[:, P:2 * P], seq(X, g, b), ALU.add).then_inc(S["t_x2"], 1)
                dve.wait_ge(S["t_x2"], n + 1)
                stat(X, g, b, S["u_stat"])

            def cross(g):
                for b in range(GB):
                    cur = GB * g + b
                    more = not (last(g) and b == GB - 1)
                    begun = not (first(g) and b == 0)
                    if more:
                        maxima(cur + 1, 0, b + 1)
                        maxima(cur + 1, 1, b + 1)
                        maxima(cur + 1, 2, b + 1)
                    if begun:
                        attend(cur - 1)
                    if more:
                        maxima(cur + 1, 3, b + 1)
                        max_parts(cur + 1, b + 1)
                    if begun:
                        residual(cur - 1, g, b - 1)

            dve.wait_ge(S["l_cb"], NG)
            for s in range(NSET):
                maxima(0, s, 0)
            max_parts(0, 0)
            groups(dve, cross)
            attend(B - 1)
            residual(B - 1, NG - 1, GB - 1)

            dve.wait_ge(S["u_stat"], B)
            moments(0, B, S["u_m1"], S["u_m2"], S["u_var"], 3, 2)
            dve.wait_ge(S["u_rstd"], 1)
            with dve.Fori(0, NG) as g:
                for b in range(GB):
                    normalise(seq(X3, g, b), seq(X, g, b), g, b).then_inc(S["u_x3"], 1)
                dve.wait_ge(S["u_x3"], GB * g + GB)
                V.tensor_reduce(mxs[:, 0, bass.ds(g, 1)], grp(X3, g), AX.X, ALU.max,
                                apply_absolute_value=True).then_inc(S["u_mx"], 1)

            n_scale = [0]

            def scales(k0, k1, unit_of):
                n_scale[0] += 1
                n, r = n_scale[0], slice(k0, k1)
                V.tensor_reduce(mx1[:, r], mxs[:, r, :], AX.X, ALU.max).then_inc(S["g_mx"], 1)
                unit_of().then_inc(S["g_unit"], 1)
                dve.wait_ge(S["g_unit"], n)
                dve.wait_ge(S["g_all"], n)
                V.scalar_tensor_tensor(out=sc0[:, r], in0=mxa[:, r], scalar=1.0 / AQ, in1=unit[:, r],
                                       op0=ALU.mult, op1=ALU.mult).then_inc(S["g_s0"], 1)
                dve.wait_ge(S["g_s0"], n)
                V.tensor_scalar(scale[:, r], sc0[:, r], 1e-12, None, ALU.max).then_inc(S["g_s"], 1)
                dve.wait_ge(S["g_s"], n)
                V.reciprocal(recip[:, r], scale[:, r]).then_inc(S["g_r"], 1)
                dve.wait_ge(S["g_r"], n)
                V.tensor_tensor(lev[:, r], recip[:, r], unit[:, r], ALU.mult).then_inc(S["g_lev"], 1)
                dve.wait_ge(S["g_lev"], n)

            dve.wait_ge(S["u_mx"], NG)
            scales(0, 1, lambda: V.memset(unit[:, 0:1], 1.0))

            def levels(g):
                if not first(g):
                    wait(dve, "a_n3", g)
                V.tensor_scalar(n3m[:, :], grp(X3, g), lev[:, 0:1], MAGIC, ALU.mult, ALU.add).then_inc(S["a_rnd"], 1)
                dve.wait_ge(S["a_rnd"], g + 1)
                if not first(g):
                    wait(dve, "a_nT", g)
                V.tensor_scalar(n3[:, :], n3m[:, :], -MAGIC, None, ALU.add).then_inc(S["a_n3"], 1)

            def largest_ug(g):
                for k, t in ((1, U), (2, G)):
                    dve.wait_ge(S["a_uc"], 6 * g + 3 * k)
                    V.tensor_reduce(mxs[:, k, bass.ds(g, 1)], grp(t, g, FW), AX.X, ALU.max,
                                    apply_absolute_value=True).then_inc(S["a_mx"], 1)

            levels(0)
            with dve.Fori(0, NG - 1) as g:
                levels(g + 1)
                largest_ug(g)
            largest_ug(NG - 1)
            dve.wait_ge(S["a_mx"], 2 * NG)
            scales(1, 3, lambda: V.tensor_copy(unit[:, 1:3], bc(scale[:, 0:1], [P, 2])))

            def gate(i, u):
                g = 2 * i + u
                dve.wait_ge(S["b_sig"], g + 1)
                wait(dve, "b_t", g)
                V.tensor_scalar(sq[:, :], sig[:, u], 65536.0, 65535.0, ALU.mult, ALU.min).then_inc(S["b_sq"], 1)
                dve.wait_ge(S["b_sq"], g + 1)
                V.tensor_tensor(grp(G, g, FW), ng[:, u], sq[:, :], ALU.mult).then_inc(S["b_t"], 1)
                dve.wait_ge(S["b_t"], g + 1)
                V.tensor_reduce(mxs[:, 3, bass.ds(g, 1)], grp(G, g, FW), AX.X, ALU.max,
                                apply_absolute_value=True).then_inc(S["b_mx"], 1)

            gate(0, 0)
            gate(0, 1)
            with dve.Fori(1, NG // 2) as i:
                gate(i, 0)
                gate(i, 1)
            dve.wait_ge(S["b_mx"], NG)
            scales(3, 4, lambda: V.tensor_scalar(unit[:, 3:4], scale[:, 2:3], 1.0 / 65536.0, None, ALU.mult))

            def product(i, u):
                g = 2 * i + u
                dve.wait_ge(S["c_tn"], g + 1)
                dve.wait_ge(S["b_un"], g + 1)
                V.tensor_tensor(grp(G, g, FW), tn[:, u], grp(UN, g, FW), ALU.mult).then_inc(S["c_o"], 1)
                dve.wait_ge(S["c_o"], g + 1)
                V.tensor_reduce(mxs[:, 4, bass.ds(g, 1)], grp(G, g, FW), AX.X, ALU.max,
                                apply_absolute_value=True).then_inc(S["c_mx"], 1)

            with dve.Fori(0, NG // 2) as i:
                product(i, 0)
                product(i, 1)
            dve.wait_ge(S["c_mx"], NG)
            scales(4, 5, lambda: V.tensor_tensor(unit[:, 4:5], scale[:, 3:4], scale[:, 1:2], ALU.mult))

            def product_levels(i, u):
                g = 2 * i + u
                V.tensor_scalar(grp(G, g, FW), grp(G, g, FW), lev[:, 4:5], MAGIC, ALU.mult, ALU.add).then_inc(S["d_rnd"], 1)
                dve.wait_ge(S["d_rnd"], g + 1)
                wait(dve, "d_y", g - 1)
                V.tensor_scalar(on[:, u], grp(G, g, FW), -MAGIC, None, ALU.add).then_inc(S["d_on"], 1)

            def result(i, u):
                g = 2 * i + u
                dve.wait_ge(S["d_y"], g + 1)
                wait(dve, "d_st%d" % u, 16 * i)
                V.scalar_tensor_tensor(out=y[:, u], in0=bank(u), scalar=scale[:, 4:5], in1=grp(X, g),
                                       op0=ALU.mult, op1=ALU.add).then_inc(S["d_yc"], 1)

            def turn(i):
                product_levels(i, 0)
                if not (isinstance(i, int) and i == 0):
                    result(i - 1, 1)
                product_levels(i, 1)
                result(i, 0)

            turn(0)
            turn(1)
            with dve.Fori(2, NG // 2) as i:
                turn(i)
            result(NG // 2 - 1, 1)


_INS = ["x", "ctx_1024", "mask_Bx1xS2_ik0", "L0_attn_W_qkv", "L0_xattn_Wq", "L0_xattn_bq", "L0_xattn_Wk",
        "L0_xattn_bk", "L0_xattn_Wv", "L0_xattn_bv", "L0_xattn_Wo", "L0_xattn_bo", "L0_ffn_w_gate",
        "L0_ffn_w_up", "L0_ffn_w_down"]
_OUTS = [((32, 128, 128), "float32")]


def kernel(**inputs):
    import numpy as _np
    import concourse.bacc as _bacc
    from concourse import mybir as _mybir
    from concourse.bass_utils import run_bass_kernel_spmd as _run

    nc = _bacc.Bacc("TRN2", target_bir_lowering=False, num_devices=1)
    arrays, args = {}, []
    for name in _INS:
        a = _np.ascontiguousarray(inputs[name])
        arrays[f"in_{name}_dram"] = a
        args.append(nc.dram_tensor(f"in_{name}_dram", a.shape, _mybir.dt.from_np(a.dtype), kind="ExternalInput").ap())
    for i, (shape, dtype) in enumerate(_OUTS):
        dt = _mybir.dt.from_np(_np.dtype(dtype))
        args.append(nc.dram_tensor(f"out_{i}_dram", shape, dt, kind="ExternalOutput").ap())
    decoder(nc, *args)
    r = _run(nc, [arrays], core_ids=[0])
    got = tuple(r.results[0][f"out_{i}_dram"] for i in range(len(_OUTS)))
    return got[0]
```

```python
from contextlib import ExitStack

import concourse.bass as bass
from concourse import mybir

ALU = mybir.AluOpType
ACT = mybir.ActivationFunctionType
F32 = mybir.dt.float32
F16 = mybir.dt.float16
BF16 = mybir.dt.bfloat16
I32 = mybir.dt.int32
I16 = mybir.dt.int16
U16 = mybir.dt.uint16
AX = mybir.AxisListType
RMAX = bass.bass_isa.ReduceOp.max

P = 128
B = 32
GB = 4
NG = B // GB
GT = GB * P
H = 16
DK = P // H
JT = 4
NSET = H // JT
RT = P // JT
CT = 4
VW = 16
EARLY = NG - 1 - GB
FC = 3
QB = 32
EPS = 1e-5
MAGIC = 12582912.0
NEG = -1.0e9
CAUSAL = -1.0e30
AQ = 32767.0


def bc(ap, shape):
    return ap.broadcast_to(shape)


def decoder(nc, x, ctx_in, mask, Wqkv, Wq, bq, Wk, bk, Wv, bv, Wo, bo, w_gate, w_up, w_down, out):
    with ExitStack() as ctx:
        def sb(name, shape, dt=F32, where=ctx):
            return where.enter_context(nc.sbuf_tensor(name, shape, dt))

        def sem(name):
            return ctx.enter_context(nc.semaphore(name))

        X = sb("X", [P, B * P])
        ident = sb("ident", [P, P])
        identb = sb("identb", [P, P], BF16)
        gateT = sb("gateT", [P, FC * P])
        upT = sb("upT", [P, FC * P])
        downT = sb("downT", [P, FC * P])
        mhalf = sb("mhalf", [P, GB])
        norms = [{name: sb("%s%d" % (name, k + 1), [P, n * GB]) for name, n in
                  (("stats", 6), ("mdif", 1), ("msum", 1), ("mdq", 1), ("sqs", 1), ("mean", 1), ("vare", 1), ("rstd", 1))}
                 for k in range(3)]
        X3 = sb("X3", [P, B * P])
        mxs = sb("mxs", [P, 5, NG])

        early = ExitStack()
        WS = sb("WS", [P, 3 * P], where=early)
        WX = sb("WX", [P, 4, P], where=early)
        WF = sb("WF", [P, 3, FC * P], where=early)
        WR = sb("WR", [P, 3 * FC * P], where=early)
        blkmax = sb("blkmax", [P, 36], where=early)
        blkscale = sb("blkscale", [P, 36], where=early)
        blkrecip = sb("blkrecip", [P, 36], where=early)
        WST = sb("WST", [P, 2 * P], where=early)
        A = sb("A", [P, P], where=early)
        WXT = sb("WXT", [P, 4, P], where=early)
        bcol = sb("bcol", [P, 3], where=early)
        borow = sb("borow", [1, P], where=early)
        bvrep = sb("bvrep", [P, P], where=early)
        cbias = sb("cbias", [P, P], where=early)
        ones = sb("ones", [P, P], where=early)
        causal = sb("causal", [P, P], where=early)
        causalb = sb("causalb", [P, P], BF16, where=early)
        M32 = sb("M32", [B, P], I32, where=early)
        MV = sb("MV", [B, P], where=early)
        nvalid = sb("nvalid", [B, 1], where=early)
        MR = sb("MR", [B, P], where=early)
        vmask = sb("vmask", [P, B], where=early)
        anyv = sb("anyv", [P, B], where=early)
        cnt1 = sb("cnt1", [P, B], where=early)
        cntr = sb("cntr", [P, B], where=early)
        vn = sb("vn", [P, B], where=early)
        bmask = sb("bmask", [P, B], where=early)
        mcol = sb("mcol", [P, 2, 2], where=early)
        sel16 = sb("sel16", [P, H], where=early)
        inj = sb("inj", [P, H, P], BF16, where=early)
        ctxg = sb("ctxg", [P, GT], where=early)
        mrow = sb("mrow", [P, B * P], where=early)
        pick = sb("pick", [P, GT], where=early)
        pickd = sb("pickd", [P, GT], where=early)
        h = sb("h", [P, GT], where=early)
        hT = sb("hT", [P, GT], where=early)
        aT = sb("aT", [P, GT], where=early)
        v1 = sb("v1", [P, GT], where=early)
        nmax = sb("nmax", [P, GB], where=early)
        pexp = sb("pexp", [P, GT], where=early)
        psum1 = sb("psum1", [P, GB], where=early)
        pinv = sb("pinv", [P, GB], where=early)
        pT = sb("pT", [P, GT], where=early)
        h2 = sb("h2", [P, GT], where=early)
        h2T = sb("h2T", [P, GT], where=early)
        cT = sb("cT", [P, GT], where=early)
        qhi = sb("qhi", [P, GT], F16, where=early)
        qlo = sb("qlo", [P, GT], F16, where=early)
        khi = sb("khi", [P, GT], F16, where=early)
        klo = sb("klo", [P, GT], F16, where=early)
        V2 = sb("V2", [P, B * P], where=early)
        VP = sb("VP", [P, 2, H, 2 * VW], where=early)
        qblk = sb("qblk", [P, 4, JT, NSET, P], F16, where=early)
        kd = sb("kd", [P, 4, NSET, P], F16, where=early)
        PT = sb("PT", [P, NSET, GT], where=early)
        nm = sb("nm", [P, 2, H], where=early)
        NM = sb("NM", [P, P], BF16, where=early)
        mT = sb("mT", [P, P], BF16, where=early)
        orec = sb("orec", [P, H], where=early)
        oun = sb("oun", [P, 2 * P], where=early)
        on_ = sb("on_", [P, P], where=early)
        oT = sb("oT", [P, P], where=early)
        early.close()

        def q_parts(g):
            if isinstance(g, int) and g == NG - 1:
                both = aT[:, :].bitcast(F16)
                return both[:, 0:GT], both[:, GT:2 * GT]
            return qhi[:, :], qlo[:, :]

        late = ctx.enter_context(ExitStack())
        FW = FC * GT
        PW = 2 * GT
        U = sb("U", [P, NG * FW], where=late)
        G = sb("G", [P, NG * FW], where=late)
        GI = G[:, :].bitcast(I32)
        n3 = sb("n3", [P, GT], where=late)
        n3m = sb("n3m", [P, GT], where=late)
        ng = sb("ng", [P, 2, FW], I32, where=late)
        sig = sb("sig", [P, 2, FW], where=late)
        sq = sb("sq", [P, 2, FW], I32, where=late)
        tn, un = ng, sq
        oq = ng
        on = sig
        y = sb("y", [P, 2, GT], where=late)
        mx1 = sb("mx1", [P, 5], where=late)
        mxa = sb("mxa", [P, 5], where=late)
        unit = sb("unit", [P, 5], where=late)
        sc0 = sb("sc0", [P, 5], where=late)
        scale = sb("scale", [P, 5], where=late)
        recip = sb("recip", [P, 5], where=late)
        lev = sb("lev", [P, 5], where=late)

        def dram(name, shape, dt):
            return nc.dram_tensor(name, shape, dt, kind="Internal").ap()

        q_dram = dram("q_dram", [B, 4, P * P], F16)
        k_dram = dram("k_dram", [B, 4, P * P], F16)
        m_dram = dram("m_dram", [B, P], F32)

        banks = ctx.enter_context(nc.psum_tensor("banks", [P, 8, GT], F32))

        def bank(n, k=1):
            return banks[:, n:n + k, :].rearrange("p k t -> p (k t)")

        names = """ld_w ld_x0 ld_x ld_ctx ld_m ld_wf
            c_set c_vp c_id c_causal c_causalb c_wz c_inj c_bcol c_bv
            w_t1 w_t1c w_a w_ac w_t2 w_t2c w_cb w_cbc
            m_val m_r m_t m_tc m_cnt m_count m_b m_vn m_st
            f_max f_sc f_rc f_mul f_rnd f_sub f_clip f_deq f_t f_tc
            s_stat s_m1 s_m2 s_var s_rstd s_h s_hT s_hTc s_a s_ac s_v s_vc s_s s_nm s_exp s_pT s_pTc s_pv s_inv s_x1
            l_stat l_m1 l_m2 l_var l_rstd l_h l_hT l_hTc ld_mr0 ld_mr l_pd l_pe l_pick l_cT l_cTc l_k l_khi l_klo l_q l_qhi l_qlo l_v l_vc l_cb l_qst l_kst
            t_ld0 t_ld1 t_ld2 t_ld3 t_lk0 t_lk1 t_lk2 t_lk3 t_sn t_max t_nhi t_nm t_mT t_mTc t_st t_exp t_pv t_rec t_ou t_tr t_o t_oT t_oTc t_wo t_x2 t_mk t_vp
            u_stat u_m1 u_m2 u_var u_rstd u_x3 u_mx
            g_mx g_all g_unit g_s0 g_s g_r g_lev
            a_rnd a_n3 a_nT a_nTc a_g a_gc a_mx
            b_u b_uc b_umx b_ng b_sig b_sq b_t b_t7 b_mx c_tn c_un c_o0 c_o1 c_o2 c_mx
            d_oq d_on d_y d_yc d_st0 d_st1""".split()
        S = {n: sem(n) for n in names}

        block = ctx.enter_context(nc.Block())
        xs = x.rearrange("b s d -> s b d")
        cs = ctx_in.rearrange("b s d -> s b d")
        os = out.rearrange("b s d -> s b d")
        X4 = X[:, :].rearrange("p (b d) -> p b d", d=P)

        def packed(d, n, j):
            return d[n].rearrange("c (j e x) -> j c e x", j=JT, e=DK)[j]

        def groups(eng, step):
            step(0)
            with eng.Fori(0, NG // 2 - 1) as i:
                step(2 * i + 1)
                step(2 * i + 2)
            step(NG - 1)

        def pipeline(eng, step, ahead=None):
            step(0, None, None)
            step(1, 0, None)
            step(2, 1, 0)
            with eng.Fori(3, NG - 1) as a:
                step(a, a - 1, a - 2)
            step(NG - 1, NG - 2, NG - 3)
            step(None, NG - 1, NG - 2)
            if ahead:
                ahead()
            step(None, None, NG - 1)

        def pairs(eng, turn):
            turn(0)
            with eng.Fori(1, NG // 2 - 1) as i:
                turn(i)
            turn(NG // 2 - 1)

        def wait(eng, name, value):
            if not (isinstance(value, int) and value <= 0):
                eng.wait_ge(S[name], value)

        def first(g):
            return isinstance(g, int) and g == 0

        def last(g):
            return isinstance(g, int) and g == NG - 1

        def seq(t, g, b):
            return t[:, bass.ds(g * GT + b * P, P)]

        def grp(t, g, w=GT):
            return t[:, bass.ds(g * w, w)]

        @block.sync
        def _(sp):
            def load_context(g):
                sp.dma_start(ctxg[:, :].rearrange("p (b d) -> p b d", d=P),
                             cs[:, bass.ds(g * GB, GB), :]).then_inc(S["ld_ctx"], 16)

            def load_x(r, name):
                sp.dma_start(X4[:, r, :], xs[:, r, :]).then_inc(S[name], 16)

            load_x(slice(0, 2 * GB), "ld_x0")
            sp.dma_start(M32[:, :], mask.rearrange("b o s -> (b o) s")).then_inc(S["ld_m"], 16)
            sp.dma_start(WS[:, :], Wqkv).then_inc(S["ld_w"], 16)
            load_context(0)
            for n, w in enumerate((Wq, Wk, Wv, Wo)):
                sp.dma_start(WX[:, n, :], w).then_inc(S["ld_w"], 16)
            for n, b_ in enumerate((bq, bk)):
                sp.dma_start(bcol[:, n:n + 1], b_.rearrange("(s j e o) -> j e s o", s=NSET, j=JT, o=1),
                             allow_slow_non_contiguous=True).then_inc(S["ld_w"], 16)
            sp.dma_start(bcol[:, 2:3], bv.rearrange("(p o) -> p o", o=1)).then_inc(S["ld_w"], 16)
            sp.dma_start(borow[:, :], bo.rearrange("(o d) -> o d", o=1)).then_inc(S["ld_w"], 16)
            for q in range(1, 4):
                load_x(slice(q * B // 4, (q + 1) * B // 4), "ld_x")
            for n, w in enumerate((w_gate, w_up)):
                sp.dma_start(WF[:, n, :].rearrange("p (c d) -> p c d", c=FC),
                             w.rearrange("(c p) d -> p c d", c=FC)).then_inc(S["ld_wf"], 16)
            sp.dma_start(WF[:, 2, :], w_down).then_inc(S["ld_wf"], 16)
            sp.wait_ge(S["m_r"], 1)
            sp.dma_start(m_dram, MR[:, :]).then_inc(S["m_st"], 16)
            sp.wait_ge(S["m_st"], 16)
            flat = m_dram.rearrange("b s -> (b s)")
            sp.dma_start(mrow[:, 0:GT], flat[0:GT].partition_broadcast(P)).then_inc(S["ld_mr0"], 16)
            sp.dma_start(mrow[:, GT:B * P], flat[GT:B * P].partition_broadcast(P)).then_inc(S["ld_mr"], 16)

            def store(d, hi_lo, g, done):
                for c in range(4):
                    sp.dma_start(d[bass.ds(g * GB, GB), c].rearrange("b (r t) -> r b t", t=P),
                                 hi_lo[c].rearrange("r (b t) -> r b t", b=GB)).then_inc(S[done], 16)

            def store_k(g):
                sp.wait_ge(S["l_klo"], g + 1)
                hi, lo = khi[:, :], klo[:, :]
                store(k_dram, (hi, lo, hi, lo), g, "l_kst")

            def store_q(g):
                sp.wait_ge(S["l_qlo"], g + 1)
                hi, lo = q_parts(g)
                store(q_dram, (hi, hi, lo, lo), g, "l_qst")

            def next_context(g):
                sp.wait_ge(S["l_cT"], g + 1)
                load_context(g + 1)

            def fill(b, n, js):
                for j in range(JT):
                    sp.dma_start(qblk[j * RT:j * RT + RT, b, j].rearrange("r s t -> r (s t)"), packed(q_dram, n, j)
                                 ).then_inc(S["t_ld%d" % b], 16)
                for j in range(js):
                    sp.dma_start(kd[j * RT:j * RT + RT, b].rearrange("r s t -> r (s t)"), packed(k_dram, n, j)
                                 ).then_inc(S["t_ld%d" % b], 16)

            next_context(0)
            store_k(0)
            with sp.Fori(0, EARLY) as g:
                next_context(g + 1)
                store_k(g + 1)
                store_q(g)

            sp.wait_ge(S["l_kst"], 64 * (EARLY + 1))
            sp.wait_ge(S["l_qst"], 64 * EARLY)
            sp.wait_ge(S["c_set"], 4)
            sp.wait_ge(S["c_wz"], 2)
            for g in range(EARLY, NG - 1):
                if g + 1 < NG - 1:
                    next_context(g + 1)
                store_k(g + 1)
                store_q(g)
                fill(g - EARLY, g - EARLY, JT)
            store_q(NG - 1)

            def fill_group(g):
                for b in range(GB):
                    sp.wait_ge(S["t_st"], NSET * (GB * (g - 1) + b) + NSET)
                    fill(b, GB * g + b, JT // 2)

            with sp.Fori(1, NG - 2) as g:
                fill_group(g)
            sp.wait_ge(S["l_kst"], 64 * NG)
            sp.wait_ge(S["l_qst"], 64 * NG)
            fill_group(NG - 2)
            fill_group(NG - 1)

            with sp.Fori(0, NG // 2) as i:
                for u in range(2):
                    sp.wait_ge(S["d_yc"], 2 * i + u + 1)
                    sp.dma_start(os[:, bass.ds(i * 2 * GB + u * GB, GB), :],
                                 y[:, u].rearrange("p (b d) -> p b d", d=P)).then_inc(S["d_st%d" % u], 16)
            sp.wait_ge(S["d_st0"], 16 * NG // 2)
            sp.wait_ge(S["d_st1"], 16 * NG // 2)

        @block.gpsimd
        def _(pool):
            nc.gpsimd.memset(ident[:, :], 0.0).then_inc(S["c_set"], 1)
            nc.gpsimd.memset(causal[:, :], 0.0).then_inc(S["c_set"], 1)
            nc.gpsimd.memset(mhalf[:, :], -0.5).then_inc(S["c_set"], 1)
            pool.wait_ge(S["c_set"], 3)
            nc.gpsimd.affine_select(out=ident[:, :], in_=ident[:, :], compare_op=ALU.not_equal, fill=1.0,
                                    base=0, pattern=[[-1, P]], channel_multiplier=1).then_inc(S["c_id"], 1)
            nc.gpsimd.affine_select(out=causal[:, :], in_=causal[:, :], compare_op=ALU.is_ge, fill=CAUSAL,
                                    base=0, pattern=[[-1, P]], channel_multiplier=1).then_inc(S["c_causal"], 1)
            nc.gpsimd.memset(qblk[:, 0:2], 0.0).then_inc(S["c_set"], 1)
            def inverse_root(k, g, after, done):
                pool.wait_ge(S[after], g + 1)
                nc.gpsimd.tensor_tensor(norms[k]["rstd"][:, :], norms[k]["vare"][:, :], mhalf[:, :], ALU.pow
                                        ).then_inc(S[done], 1)

            def picker(g):
                four = [P, GB, P]
                idb = bc(ident[:, :].unsqueeze(1), four)
                pickd4, pick4 = (t[:, :].rearrange("p (b k) -> p b k", b=GB) for t in (pickd, pick))
                wait(pool, "l_pick", g)
                nc.gpsimd.tensor_tensor(pickd4, bc(vn[:, bass.ds(g * GB, GB)].unsqueeze(2), four), idb,
                                        ALU.subtract).then_inc(S["l_pd"], 1)
                pool.wait_ge(S["l_pd"], g + 1)
                nc.gpsimd.tensor_tensor(pickd[:, :], pickd[:, :], grp(mrow, g), ALU.mult).then_inc(S["l_pe"], 1)
                pool.wait_ge(S["l_pe"], g + 1)
                wait(pool, "l_cT", g)
                nc.gpsimd.tensor_tensor(pick4, pickd4, idb, ALU.add).then_inc(S["l_pick"], 1)

            def add_constant(g):
                pool.wait_ge(S["l_h"], GB * g + GB)
                xg = grp(X, g).rearrange("p (b d) -> p b d", d=P)
                nc.gpsimd.tensor_tensor(xg, xg, bc(cbias[:, :].unsqueeze(1), [P, GB, P]), ALU.add).then_inc(S["l_cb"], 1)

            inverse_root(0, 0, "s_var", "s_rstd")

            def step(a, b, c):
                if a is not None and not last(a):
                    inverse_root(0, a + 1, "s_var", "s_rstd")
                if first(a):
                    pool.wait_ge(S["m_vn"], 1)
                    pool.wait_ge(S["w_cbc"], 1)
                    pool.wait_ge(S["ld_mr0"], 16)
                    picker(0)
                    pool.wait_ge(S["ld_mr"], 16)
                if c is not None:
                    add_constant(c)
                if b is not None and not last(b):
                    picker(b + 1)
                if b is not None:
                    inverse_root(1, b, "l_var", "l_rstd")

            pipeline(pool, step)

            def fill(b, n):
                for j in range(JT // 2, JT):
                    nc.gpsimd.dma_start(kd[j * RT:j * RT + RT, b].rearrange("r s t -> r (s t)"), packed(k_dram, n, j)
                                        ).then_inc(S["t_lk%d" % b], 16)

            pool.wait_ge(S["l_vc"], NG)
            pool.wait_ge(S["c_vp"], 1)

            def mask_columns(g):
                for b in range(GB):
                    if not (first(g) and b < 2):
                        pool.wait_ge(S["t_pv"], NSET * (GB * g + b) - NSET)
                    nc.gpsimd.tensor_copy(mcol[:, b % 2, 0:1], vmask[:, bass.ds(GB * g + b, 1)]).then_inc(S["t_mk"], 1)
                    nc.gpsimd.tensor_copy(mcol[:, b % 2, 1:2], bmask[:, bass.ds(GB * g + b, 1)]).then_inc(S["t_mk"], 1)
                    src = seq(V2, g, b).rearrange("p (a k j e) -> p a k j e", a=2, k=2, j=JT)
                    dst = VP[:, b % 2].rearrange("p (a k j) c -> p a k j c", a=2, k=2)
                    for k in range(2):
                        nc.gpsimd.tensor_copy(dst[:, :, k, :, VW * k:VW * k + DK], src[:, :, k]).then_inc(S["t_vp"], 1)
                    if first(g) and b == 1:
                        pool.wait_ge(S["l_kst"], 64 * NG)
                    if not (first(g) and b == 0) and not (last(g) and b > 0):
                        pool.wait_ge(S["t_st"], NSET * (GB * g + b))
                        fill((b + 3) % GB, GB * g + b + 3)
                    if b == 2 and not first(g):
                        inverse_root(2, g - 1, "u_var", "u_rstd")

            groups(pool, mask_columns)

            inverse_root(2, NG - 1, "u_var", "u_rstd")
            def over_partitions(n, k0, k1):
                pool.wait_ge(S["g_mx"], n)
                nc.gpsimd.partition_all_reduce(mxa[:, k0:k1], mx1[:, k0:k1], P, RMAX).then_inc(S["g_all"], 1)

            over_partitions(1, 0, 1)
            over_partitions(2, 1, 2)

            def gated(i):
                for u in range(1 if isinstance(i, int) and i == NG // 2 - 1 else 2):
                    g = 2 * i + u
                    pool.wait_ge(S["b_sq"], g + 1)
                    pool.wait_ge(S["b_ng"], g + 1)
                    nc.gpsimd.tensor_tensor(grp(GI, g, FW), ng[:, u], sq[:, u], ALU.mult).then_inc(S["b_t"], 1)

            pairs(pool, gated)
            over_partitions(3, 2, 4)

            with pool.Fori(0, NG // 2) as i:
                pool.wait_ge(S["c_tn"], 2 * i + 1)
                pool.wait_ge(S["c_un"], 2 * i + 1)
                nc.gpsimd.tensor_tensor(GI[:, bass.ds(i * 2 * FW, PW)], tn[:, 0, 0:PW], un[:, 0, 0:PW], ALU.mult
                                        ).then_inc(S["c_o0"], 1)
            over_partitions(4, 4, 5)

        @block.tensor
        def _(pe):
            pe.wait_ge(S["c_id"], 1)
            pe.wait_ge(S["ld_w"], 16 * 9)
            pe.transpose(bank(0)[:, 0:P], WS[:, 0:P], ident[:, :])
            pe.transpose(bank(0)[:, P:2 * P], WS[:, P:2 * P], ident[:, :]).then_inc(S["w_t1"], 1)
            for n in range(4):
                m = pe.transpose(bank(2)[:, n * P:(n + 1) * P], WX[:, n, :], ident[:, :])
            m.then_inc(S["w_t2"], 1)
            pe.wait_ge(S["w_t1c"], 1)
            pe.matmul(bank(1)[:, 0:P], WST[:, 0:P], WST[:, P:2 * P], start=True, stop=True).then_inc(S["w_a"], 1)
            pe.wait_ge(S["w_t2c"], 3)
            pe.wait_ge(S["c_bv"], 1)
            pe.wait_ge(S["c_wz"], 1)
            pe.matmul(bank(3)[:, 0:P], bvrep[:, :], WXT[:, 3, :], start=True, stop=False)
            pe.matmul(bank(3)[:, 0:P], ones[0:1, :], borow[:, :], start=False, stop=True).then_inc(S["w_cb"], 1)
            pe.wait_ge(S["m_val"], 1)
            pe.transpose(bank(4)[:, 0:B], MV[:, :], ident[0:B, 0:B]).then_inc(S["m_t"], 1)
            pe.wait_ge(S["m_tc"], 1)
            pe.matmul(bank(5)[:, 0:B], ones[:, :], vmask[:, :], start=True, stop=True).then_inc(S["m_cnt"], 1)
            pe.wait_ge(S["w_ac"], 1)
            pe.wait_ge(S["w_cbc"], 1)
            pe.wait_ge(S["m_b"], 1)

            def transposes(n, src):
                for b in range(GB):
                    m = pe.transpose(bank(n)[:, b * P:(b + 1) * P], src(b), ident[:, :])
                return m

            def products(n, lhs, rhs):
                for b in range(GB):
                    r = slice(b * P, (b + 1) * P)
                    m = pe.matmul(bank(n)[:, r], lhs(r), rhs(r), start=True, stop=True)
                return m

            pe.wait_ge(S["c_causalb"], 1)

            def turn_rows2(c):
                pe.wait_ge(S["l_h"], GB * c + GB)
                transposes(5, lambda q: h2[:, q * P:(q + 1) * P]).then_inc(S["l_hT"], 1)

            def step(a, b, c):
                if b is not None:
                    pe.wait_ge(S["s_exp"], GB * b + GB)
                    wait(pe, "l_hTc", b - 1)
                    transposes(5, lambda q: pexp[:, q * P:(q + 1) * P]).then_inc(S["s_pT"], 1)
                if a is not None:
                    pe.wait_ge(S["s_h"], GB * a + GB)
                    wait(pe, "s_hTc", a)
                    transposes(0, lambda q: h[:, q * P:(q + 1) * P]).then_inc(S["s_hT"], 1)
                if b is not None:
                    pe.wait_ge(S["ld_ctx"], 16 * b + 16)
                    pe.wait_ge(S["l_pick"], b + 1)
                    wait(pe, "l_vc", b)
                    products(1, lambda r: ctxg[:, r], lambda r: pick[:, r]).then_inc(S["l_cT"], 1)
                if a is not None:
                    pe.wait_ge(S["s_hTc"], a + 1)
                    wait(pe, "s_ac", a)
                    pe.matmul(bank(2), A[:, :], hT[:, :], start=True, stop=True).then_inc(S["s_a"], 1)
                if b is not None:
                    pe.wait_ge(S["s_pTc"], b + 1)
                    pe.wait_ge(S["s_vc"], b + 1)
                    wait(pe, "l_qlo", b - 1)
                    products(6, lambda r: pT[:, r], lambda r: v1[:, r]).then_inc(S["s_pv"], 1)
                if a is not None:
                    wait(pe, "s_vc", a)
                    products(3, lambda r: hT[:, r], lambda r: WS[:, 2 * P:3 * P]).then_inc(S["s_v"], 1)
                    pe.wait_ge(S["s_ac"], a + 1)
                    wait(pe, "s_exp", GB * a)
                    pe.matmul(bank(4).rearrange("p (q m) -> p q m", m=P), identb[:, :],
                              bc(causalb[:, :].unsqueeze(1), [P, GB, P]), start=True, stop=False, skip_group_check=True)
                    for q in range(GB):
                        r = slice(q * P, (q + 1) * P)
                        m = pe.matmul(bank(4)[:, r], aT[:, r], hT[:, r], start=False, stop=(q == GB - 1),
                                      skip_group_check=True)
                    m.then_inc(S["s_s"], 1)
                if b is not None:
                    pe.wait_ge(S["l_cTc"], b + 1)
                    wait(pe, "l_klo", b)
                    pe.matmul(bank(7), WXT[:, 1, :], cT[:, :], start=True, stop=True).then_inc(S["l_k"], 1)
                if c is not None and not last(c):
                    pe.wait_ge(S["s_pTc"], b + 1)
                    turn_rows2(c)
                if b is not None:
                    products(1, lambda r: cT[:, r], lambda r: WXT[:, 2, :]).then_inc(S["l_v"], 1)
                if c is not None:
                    pe.wait_ge(S["l_hTc"], c + 1)
                    if b is not None:
                        pe.wait_ge(S["s_x1"], GB * b + GB)
                    pe.matmul(bank(6), WXT[:, 0, :], h2T[:, :], start=True, stop=True).then_inc(S["l_q"], 1)

            def scores_q(n, s, b):
                if not (isinstance(n, int) and NSET * n + s < 2):
                    pe.wait_ge(S["t_max"], NSET * n + s - 1)
                for j in range(JT):
                    m = pe.matmul(bank(s % 2)[:, j * P:(j + 1) * P], qblk[:, b % GB, j, s, :], kd[:, b % GB, s, :],
                                  start=True, stop=True)
                m.then_inc(S["t_sn"], 1)

            def scores_k(n, s, b):
                if not (isinstance(n, int) and NSET * n + s < 2):
                    pe.wait_ge(S["t_exp"], NSET * n + s - 1)
                pe.matmul(bank(2 + s % 2).rearrange("p (j t) -> p j t", j=JT), kd[:, b % GB, s, :], qblk[:, b % GB, :, s, :],
                          start=True, stop=False, skip_group_check=True)
                for j in range(JT):
                    m = pe.matmul(bank(2 + s % 2)[:, j * P:(j + 1) * P], inj[:, JT * s + j, :], mT[:, :],
                                  start=False, stop=(j == JT - 1), skip_group_check=True)
                m.then_inc(S["t_st"], 1)

            def pv(n, s, b):
                pe.wait_ge(S["t_exp"], NSET * n + s + 1)
                for j in range(JT):
                    m = pe.matmul(bank(4 + b % 2)[RT * j:RT * j + RT, s // 2 * P:s // 2 * P + P],
                                  VP[:, b % 2, JT * s + j, :], PT[:, s, j * P:(j + 1) * P],
                                  start=(s % 2 == 0), stop=(s % 2 == 1), skip_group_check=True,
                                  tile_position=(0, RT * j))
                m.then_inc(S["t_pv"], 1)

            def max_rows(n):
                pe.wait_ge(S["t_nm"], n + 1)
                wait(pe, "t_mTc", n)
                pe.transpose(bank(6).bitcast(BF16)[:, 0:P], NM[:, :], identb[:, :]).then_inc(S["t_mT"], 1)

            def queries(n):
                pe.wait_ge(S["t_ou"], n + 1)
                wait(pe, "t_x2", n)
                for a in range(2):
                    m = pe.transpose(bank(7)[:, (2 + a) * P:(3 + a) * P], oun[:, a * P:(a + 1) * P], ident[:, :])
                m.then_inc(S["t_tr"], 1)

            def turn(n):
                pe.wait_ge(S["t_o"], 2 * n + 2)
                pe.transpose(bank(7)[:, 0:P], on_[:, :], ident[:, :]).then_inc(S["t_oT"], 1)

            def project(n):
                pe.wait_ge(S["t_oTc"], n + 1)
                pe.matmul(bank(7)[:, P:2 * P], oT[:, :], WXT[:, 3, :], start=True, stop=True).then_inc(S["t_wo"], 1)

            def first_scores():
                pe.wait_ge(S["c_wz"], 5)
                pe.wait_ge(S["s_hTc"], NG)
                pe.wait_ge(S["l_vc"], NG)
                pe.wait_ge(S["t_ld0"], 128)
                scores_q(0, 0, 0)
                scores_q(0, 1, 0)
                turn_rows2(NG - 1)
                scores_q(0, 2, 0)
                scores_q(0, 3, 0)

            pipeline(pe, step, first_scores)

            pe.wait_ge(S["s_exp"], GB * NG)
            pe.wait_ge(S["l_qlo"], NG)
            pe.wait_ge(S["l_klo"], NG)
            pe.wait_ge(S["l_hTc"], NG)
            pe.wait_ge(S["c_inj"], 2)

            def cross(g):
                for b in range(GB):
                    cur = GB * g + b
                    more = not (last(g) and b == GB - 1)
                    one, two = not (first(g) and b < 1), not (first(g) and b < 2)
                    if more:
                        slot, k = (b + 1) % GB, g + (b + 1) // GB
                        pe.wait_ge(S["t_ld%d" % slot], 96 * k + 128)
                        wait(pe, "t_lk%d" % slot, 32 * k)
                        scores_q(cur + 1, 0, b + 1)
                        scores_q(cur + 1, 1, b + 1)
                    if one:
                        pv(cur - 1, 2, b - 1)
                    pe.wait_ge(S["t_mTc"], cur + 1)
                    scores_k(cur, 0, b)
                    if two:
                        turn(cur - 2)
                    scores_k(cur, 1, b)
                    if more:
                        scores_q(cur + 1, 2, b + 1)
                    if one:
                        pv(cur - 1, 3, b - 1)
                    if more:
                        scores_q(cur + 1, 3, b + 1)
                    if two:
                        project(cur - 2)
                    scores_k(cur, 2, b)
                    pe.wait_ge(S["t_vp"], 2 * cur + 2)
                    if two:
                        wait(pe, "t_ou", cur - 1)
                    pv(cur, 0, b)
                    scores_k(cur, 3, b)
                    pv(cur, 1, b)
                    if more:
                        max_rows(cur + 1)
                    if one:
                        queries(cur - 1)

            max_rows(0)
            groups(pe, cross)
            pv(B - 1, 2, GB - 1)
            turn(B - 2)
            pv(B - 1, 3, GB - 1)
            project(B - 2)
            queries(B - 1)
            turn(B - 1)
            project(B - 1)

            pe.wait_ge(S["t_x2"], B)
            pe.wait_ge(S["f_deq"], 1)
            for m_ in range(3):
                for c in range(FC):
                    w = WR[:, m_ * FC * P + c * P:m_ * FC * P + (c + 1) * P]
                    m = pe.transpose(bank(m_)[:, c * P:(c + 1) * P], w, ident[:, :])
            m.then_inc(S["f_t"], 1)
            pe.wait_ge(S["f_tc"], 3)

            def turn_levels(g, u):
                pe.wait_ge(S["a_n3"], g + 1)
                wait(pe, "a_nTc", g - 1)
                transposes(u, lambda b: n3[:, b * P:(b + 1) * P]).then_inc(S["a_nT"], 1)

            def hidden(g, u, w, read, done):
                for k in range(FC):
                    wait(pe, read, FC * g + k - 5)
                    pe.matmul(bank(2 + FC * u + k), w[:, k * P:k * P + P], grp(X3, g),
                              start=True, stop=True).then_inc(S[done], 1)

            def gate_turn(i):
                turn_levels(2 * i + 1, 1)
                pe.wait_ge(S["a_nTc"], 2 * i + 1)
                hidden(2 * i, 0, gateT, "a_gc", "a_g")
                if not (isinstance(i, int) and i == NG // 2 - 1):
                    turn_levels(2 * i + 2, 0)
                pe.wait_ge(S["a_nTc"], 2 * i + 2)
                hidden(2 * i + 1, 1, gateT, "a_gc", "a_g")

            turn_levels(0, 0)
            pairs(pe, gate_turn)

            pe.wait_ge(S["a_gc"], FC * NG)

            def up_turn(i):
                for u in range(2):
                    hidden(2 * i + u, u, upT, "b_uc", "b_u")

            pairs(pe, up_turn)

            def down(i, u, begun):
                g = 2 * i + u
                pe.wait_ge(S["d_on"], g + 1)
                if begun:
                    pe.wait_ge(S["d_yc"], g - 1)
                for b in range(GB):
                    for c in range(FC):
                        m = pe.matmul(bank(u)[:, b * P:(b + 1) * P], on[:, u, c * GT + b * P:c * GT + b * P + P],
                                      downT[:, c * P:(c + 1) * P], start=(c == 0), stop=(c == FC - 1))
                m.then_inc(S["d_y"], 1)

            down(0, 0, False)
            down(0, 1, False)
            with pe.Fori(1, NG // 2) as i:
                down(i, 0, True)
                down(i, 1, True)

        @block.scalar
        def _(act):
            act.preload_act_table(ACT.Exp)
            act.wait_ge(S["w_t1"], 1)
            act.activation(WST[:, :], bank(0)[:, 0:2 * P], ACT.Copy).then_inc(S["w_t1c"], 1)
            act.wait_ge(S["w_t2"], 1)
            for n, c in ((0, float(DK) ** -0.5), (1, 1.0)):
                act.activation(WXT[:, n, :].rearrange("p (j e s) -> p s j e", j=JT, s=NSET),
                               bank(2)[:, n * P:(n + 1) * P].rearrange("p (s j e) -> p s j e", j=JT, s=NSET),
                               ACT.Copy, scale=c).then_inc(S["w_t2c"], 1)
            act.activation(WXT[:, 2:4, :].rearrange("p n d -> p (n d)"), bank(2)[:, 2 * P:4 * P], ACT.Copy).then_inc(S["w_t2c"], 1)
            act.wait_ge(S["w_a"], 1)
            act.activation(A[:, :], bank(1)[:, 0:P], ACT.Copy, scale=float(P) ** -0.5).then_inc(S["w_ac"], 1)
            act.wait_ge(S["c_bcol"], 1)

            def step(a, b, c):
                if b is not None:
                    act.wait_ge(S["s_pT"], b + 1)
                    wait(act, "s_pv", b)
                    act.activation(pT[:, :], bank(5), ACT.Copy).then_inc(S["s_pTc"], 1)
                if a is not None:
                    act.wait_ge(S["s_hT"], a + 1)
                    wait(act, "s_s", a)
                    act.activation(hT[:, :], bank(0), ACT.Copy).then_inc(S["s_hTc"], 1)
                if b is not None:
                    act.wait_ge(S["l_cT"], b + 1)
                    wait(act, "l_v", b)
                    act.activation(cT[:, :], bank(1), ACT.Copy).then_inc(S["l_cTc"], 1)
                if a is not None:
                    act.wait_ge(S["s_a"], a + 1)
                    act.activation(aT[:, :], bank(2), ACT.Copy).then_inc(S["s_ac"], 1)
                    act.wait_ge(S["s_v"], a + 1)
                    wait(act, "s_pv", a)
                    act.activation(v1[:, :], bank(3), ACT.Copy).then_inc(S["s_vc"], 1)
                if b is not None:
                    act.wait_ge(S["l_k"], b + 1)
                    wait(act, "l_kst", 64 * b)
                    act.activation(khi[:, :], bank(7), ACT.Identity, bias=bcol[:, 1:2]).then_inc(S["l_khi"], 1)
                if c is not None:
                    act.wait_ge(S["l_hT"], c + 1)
                    wait(act, "l_q", c)
                    act.activation(h2T[:, :], bank(5), ACT.Copy).then_inc(S["l_hTc"], 1)
                if a is not None:
                    act.wait_ge(S["s_nm"], a + 1)
                    wait(act, "s_pT", a)
                    wait(act, "s_inv", a)
                    for b_ in range(GB):
                        r = slice(b_ * P, (b_ + 1) * P)
                        act.activation(pexp[:, r], bank(4)[:, r], ACT.Exp, bias=nmax[:, b_:b_ + 1],
                                       accum_out=psum1[:, b_:b_ + 1]).then_inc(S["s_exp"], 1)
                if b is not None:
                    act.wait_ge(S["l_v"], b + 1)
                    act.activation(grp(V2, b), bank(1), ACT.Copy).then_inc(S["l_vc"], 1)
                if c is not None:
                    act.wait_ge(S["l_q"], c + 1)
                    if last(c):
                        act.wait_ge(S["s_s"], NG)
                    else:
                        wait(act, "l_qst", 64 * c)
                    act.activation(q_parts(c)[0], bank(6), ACT.Identity, bias=bcol[:, 0:1]).then_inc(S["l_qhi"], 1)

            pipeline(act, step)

            def max_copy(n):
                act.wait_ge(S["t_mT"], n + 1)
                wait(act, "t_st", NSET * n)
                act.activation(mT[:, :], bank(6).bitcast(BF16)[:, 0:P], ACT.Copy).then_inc(S["t_mTc"], 1)

            def out_copy(n, b):
                act.wait_ge(S["t_pv"], NSET * n + NSET)
                wait(act, "t_tr", n)
                act.activation(oun[:, :], bank(4 + b % 2)[:, 0:2 * P], ACT.Copy).then_inc(S["t_ou"], 1)

            def turn_copy(n):
                act.wait_ge(S["t_oT"], n + 1)
                wait(act, "t_wo", n)
                act.activation(oT[:, :], bank(7)[:, 0:P], ACT.Copy).then_inc(S["t_oTc"], 1)

            def probs(g):
                for b in range(GB):
                    n = GB * g + b
                    for s in range(NSET):
                        if s == 0:
                            act.wait_ge(S["t_mk"], 2 * n + 2)
                        act.wait_ge(S["t_st"], NSET * n + s + 1)
                        if not (first(g) and b == 0):
                            act.wait_ge(S["t_pv"], NSET * n - NSET + s + 1)
                        act.activation(PT[:, s, :], bank(2 + s % 2), ACT.Exp, bias=mcol[:, b % 2, 1:2],
                                       scale=mcol[:, b % 2, 0:1]).then_inc(S["t_exp"], 1)
                        if s == 0 and not (first(g) and b < 2):
                            turn_copy(n - 2)
                        if s == 1 and not (first(g) and b == 0):
                            out_copy(n - 1, b - 1)
                    if not (last(g) and b == GB - 1):
                        max_copy(n + 1)

            max_copy(0)
            groups(act, probs)
            turn_copy(B - 2)
            out_copy(B - 1, B - 1)
            turn_copy(B - 1)

            act.wait_ge(S["f_t"], 1)
            for n, w in enumerate((gateT, upT, downT)):
                act.activation(w[:, :], bank(n)[:, 0:FC * P], ACT.Copy).then_inc(S["f_tc"], 1)

            def levels_copy(g, u):
                act.wait_ge(S["a_nT"], g + 1)
                act.activation(grp(X3, g), bank(u), ACT.Copy).then_inc(S["a_nTc"], 1)

            def hidden_copy(t, g, u, ready, done):
                for k in range(FC):
                    act.wait_ge(S[ready], FC * g + k + 1)
                    act.activation(t[:, bass.ds(g * FW + k * GT, GT)], bank(2 + FC * u + k), ACT.Copy
                                   ).then_inc(S[done], 1)

            def gate_turn(i):
                levels_copy(2 * i + 1, 1)
                hidden_copy(G, 2 * i, 0, "a_g", "a_gc")
                if not (isinstance(i, int) and i == NG // 2 - 1):
                    levels_copy(2 * i + 2, 0)
                hidden_copy(G, 2 * i + 1, 1, "a_g", "a_gc")

            levels_copy(0, 0)
            pairs(act, gate_turn)
            act.preload_act_table(ACT.Sigmoid)

            act.wait_ge(S["g_lev"], 2)

            def sigmoid_turn(i):
                for u in range(2):
                    g = 2 * i + u
                    wait(act, "b_t", g - 1)
                    act.activation(ng[:, u], grp(G, g, FW), ACT.Copy, scale=lev[:, 1:2]).then_inc(S["b_ng"], 1)
                    act.wait_ge(S["b_ng"], g + 1)
                    wait(act, "b_sq", g - 1)
                    act.activation(sig[:, u], ng[:, u], ACT.Sigmoid, scale=scale[:, 1:2]).then_inc(S["b_sig"], 1)
                    hidden_copy(U, g, u, "b_u", "b_uc")

            pairs(act, sigmoid_turn)

            act.wait_ge(S["g_lev"], 3)

            def product_turn(i):
                for u in range(2):
                    g = 2 * i + u
                    for used in (("c_o0", "c_o2"), ("c_o1",))[u]:
                        wait(act, used, i)
                    act.activation(tn[:, u], grp(GI, g, FW), ACT.Copy, scale=lev[:, 3:4]).then_inc(S["c_tn"], 1)
                    act.activation(un[:, u], grp(U, g, FW), ACT.Copy, scale=lev[:, 2:3]).then_inc(S["c_un"], 1)

            pairs(act, product_turn)

            act.wait_ge(S["g_lev"], 4)

            def levels_turn(i):
                for u in range(2):
                    g = 2 * i + u
                    wait(act, "d_on", g - 1)
                    act.activation(oq[:, u], grp(GI, g, FW), ACT.Copy, scale=lev[:, 4:5]).then_inc(S["d_oq"], 1)

            pairs(act, levels_turn)

        @block.vector
        def _(dve):
            V = nc.vector
            V.memset(ones[:, :], 1.0).then_inc(S["c_wz"], 1)
            V.memset(qblk[:, 2:4], 0.0).then_inc(S["c_wz"], 1)
            V.memset(NM[:, :], 0.0).then_inc(S["c_wz"], 1)
            V.memset(VP[:, :, :, :], 0.0).then_inc(S["c_wz"], 1)
            dve.wait_ge(S["c_id"], 1)
            V.tensor_copy(identb[:, :], ident[:, :]).then_inc(S["c_wz"], 1)
            dve.wait_ge(S["c_wz"], 4)
            for k in range(2):
                heads = VP[:, :, :, :].rearrange("p u (a k j) c -> p k (u a) j c", a=2, k=2)[:, k]
                m = V.memset(heads[:, :, :, VW * k + DK:VW * k + DK + 1], 1.0)
            m.then_inc(S["c_vp"], 1)
            dve.wait_ge(S["c_causal"], 1)
            V.tensor_copy(causalb[:, :], causal[:, :]).then_inc(S["c_causalb"], 1)
            V.tensor_tensor(sel16[:, :], ident[:, 0:H], ident[:, H:2 * H], ALU.add).then_inc(S["c_inj"], 1)
            dve.wait_ge(S["c_inj"], 1)
            V.tensor_copy(inj[:, :, :], bc(sel16[:, :].unsqueeze(2), [P, H, P])).then_inc(S["c_inj"], 1)
            dve.wait_ge(S["ld_m"], 16)
            V.tensor_scalar(MV[:, :], M32[:, :], 0.0, None, ALU.not_equal).then_inc(S["m_val"], 1)
            dve.wait_ge(S["m_val"], 1)
            V.tensor_reduce(nvalid[:, :], MV[:, :], AX.X, ALU.max).then_inc(S["m_val"], 1)
            dve.wait_ge(S["m_val"], 2)
            V.tensor_scalar(MR[:, :], MV[:, :], 0.0, nvalid[:, 0:1], ALU.is_equal, ALU.mult).then_inc(S["m_r"], 1)

            def small_setup():
                dve.wait_ge(S["ld_w"], 16 * 9)
                V.tensor_scalar(bcol[:, 0:1], bcol[:, 0:1], float(DK) ** -0.5, None, ALU.mult).then_inc(S["c_bcol"], 1)
                V.tensor_scalar(bvrep[:, :], ones[:, :], bcol[:, 2:3], None, ALU.mult).then_inc(S["c_bv"], 1)
                dve.wait_ge(S["m_t"], 1)
                V.tensor_copy(vmask[:, :], bank(4)[:, 0:B]).then_inc(S["m_tc"], 1)
                dve.wait_ge(S["m_cnt"], 1)
                V.tensor_scalar(anyv[:, :], bank(5)[:, 0:B], 1.0, -NEG, ALU.min, ALU.mult).then_inc(S["m_count"], 1)
                V.tensor_scalar(cnt1[:, :], bank(5)[:, 0:B], 1.0, None, ALU.max).then_inc(S["m_count"], 1)
                dve.wait_ge(S["m_count"], 2)
                V.reciprocal(cntr[:, :], cnt1[:, :]).then_inc(S["m_count"], 1)
                dve.wait_ge(S["m_count"], 3)
                V.tensor_tensor(vn[:, :], vmask[:, :], cntr[:, :], ALU.mult).then_inc(S["m_vn"], 1)
                dve.wait_ge(S["m_count"], 1)
                V.scalar_tensor_tensor(out=bmask[:, :], in0=vmask[:, :], scalar=-1.0, in1=anyv[:, :],
                                       op0=ALU.add, op1=ALU.mult).then_inc(S["m_b"], 1)
                dve.wait_ge(S["w_cb"], 1)
                V.tensor_copy(cbias[:, :], bank(3)[:, 0:P]).then_inc(S["w_cbc"], 1)

            def stat(k, g, b, s):
                V.bn_stats(norms[k]["stats"][:, 6 * b:6 * b + 6], seq(X, g, b)).then_inc(s, 1)

            def moments(k, g, s_1, s_2, s_3):
                N = norms[k]
                e = N["stats"][:, :].rearrange("p (b f) -> p b f", f=6)
                V.tensor_tensor(N["mdif"][:, :], e[:, :, 1], e[:, :, 4], ALU.subtract).then_inc(S[s_1], 1)
                V.tensor_tensor(N["msum"][:, :], e[:, :, 1], e[:, :, 4], ALU.add).then_inc(S[s_1], 1)
                V.scalar_tensor_tensor(out=N["sqs"][:, :], in0=e[:, :, 2], scalar=P * EPS, in1=e[:, :, 5],
                                       op0=ALU.add, op1=ALU.add).then_inc(S[s_1], 1)
                dve.wait_ge(S[s_1], 3 * g + 3)
                V.tensor_scalar(N["mean"][:, :], N["msum"][:, :], 0.5, None, ALU.mult).then_inc(S[s_2], 1)
                V.scalar_tensor_tensor(out=N["mdq"][:, :], in0=N["mdif"][:, :], scalar=0.25, in1=N["mdif"][:, :],
                                       op0=ALU.mult, op1=ALU.mult).then_inc(S[s_2], 1)
                dve.wait_ge(S[s_2], 2 * g + 2)
                V.scalar_tensor_tensor(out=N["vare"][:, :], in0=N["sqs"][:, :], scalar=1.0 / P, in1=N["mdq"][:, :],
                                       op0=ALU.mult, op1=ALU.add).then_inc(S[s_3], 1)

            def normalise(k, dst, g, b):
                return V.tensor_scalar(dst, seq(X, g, b), norms[k]["mean"][:, b:b + 1], norms[k]["rstd"][:, b:b + 1],
                                       ALU.subtract, ALU.mult)

            def stat1(g):
                for b in range(GB):
                    stat(0, g, b, S["s_stat"])
                dve.wait_ge(S["s_stat"], GB * g + GB)
                moments(0, g, "s_m1", "s_m2", "s_var")

            def rows1(g):
                dve.wait_ge(S["s_rstd"], g + 1)
                dve.wait_ge(S["s_m2"], 2 * g + 2)
                wait(dve, "s_hT", g)
                for b in range(GB):
                    normalise(0, h[:, b * P:(b + 1) * P], g, b).then_inc(S["s_h"], 1)

            dve.wait_ge(S["ld_x0"], 16)
            stat1(0)
            rows1(0)
            small_setup()

            W3 = WF[:, :, :].rearrange("p m (k e) -> p (m k) e", e=QB)
            R3 = WR[:, :].rearrange("p (k e) -> p k e", e=QB)
            wide = [P, 3 * FC * P // QB, QB]
            WR1 = WR[:, :]

            def weight_scales():
                dve.wait_ge(S["ld_wf"], 48)
                V.tensor_reduce(blkmax[:, :], W3, AX.X, ALU.max, apply_absolute_value=True).then_inc(S["f_max"], 1)
                dve.wait_ge(S["f_max"], 1)
                V.tensor_scalar(blkscale[:, :], blkmax[:, :], 1.0 / 7.0, 1e-12, ALU.mult, ALU.max).then_inc(S["f_sc"], 1)
                dve.wait_ge(S["f_sc"], 1)
                V.reciprocal(blkrecip[:, :], blkscale[:, :]).then_inc(S["f_rc"], 1)

                dve.wait_ge(S["f_rc"], 1)
                V.tensor_tensor(R3, W3, bc(blkrecip[:, :].unsqueeze(2), wide), ALU.mult).then_inc(S["f_mul"], 1)

            def weight_levels():
                dve.wait_ge(S["f_mul"], 1)
                V.tensor_scalar(WR1, WR1, MAGIC, None, ALU.add).then_inc(S["f_rnd"], 1)
                dve.wait_ge(S["f_rnd"], 1)
                V.tensor_scalar(WR1, WR1, -MAGIC, None, ALU.add).then_inc(S["f_sub"], 1)
                dve.wait_ge(S["f_sub"], 1)
                V.tensor_scalar(WR1, WR1, 7.0, -8.0, ALU.min, ALU.max).then_inc(S["f_clip"], 1)

            def weight_values():
                dve.wait_ge(S["f_clip"], 1)
                V.tensor_tensor(R3, R3, bc(blkscale[:, :].unsqueeze(2), wide), ALU.mult).then_inc(S["f_deq"], 1)

            def rows2(c):
                dve.wait_ge(S["l_rstd"], c + 1)
                wait(dve, "l_hT", c)
                for q in range(GB):
                    normalise(1, h2[:, q * P:(q + 1) * P], c, q).then_inc(S["l_h"], 1)

            def step(a, b, c):
                if a is not None and not last(a):
                    stat1(a + 1)
                if c is not None and not last(c):
                    rows2(c)
                if a is not None and not last(a):
                    rows1(a + 1)
                if first(a):
                    weight_scales()
                if b is not None:
                    wait(dve, "s_x1", GB * b)
                    dve.wait_ge(S["s_exp"], GB * b + GB)
                    V.reciprocal(pinv[:, :], psum1[:, :]).then_inc(S["s_inv"], 1)
                    if first(b):
                        weight_levels()
                    dve.wait_ge(S["s_pv"], b + 1)
                    dve.wait_ge(S["s_inv"], b + 1)
                    for q in range(GB):
                        V.scalar_tensor_tensor(out=seq(X, b, q), in0=bank(6)[:, q * P:(q + 1) * P],
                                               scalar=pinv[:, q:q + 1], in1=seq(X, b, q),
                                               op0=ALU.mult, op1=ALU.add).then_inc(S["s_x1"], 1)
                if a is not None:
                    dve.wait_ge(S["s_s"], a + 1)
                    wait(dve, "s_exp", GB * a)
                    if b is not None:
                        dve.wait_ge(S["s_x1"], GB * b + GB)
                    V.tensor_reduce(nmax[:, :], bank(4).rearrange("p (q m) -> p q m", m=P), AX.X, ALU.max,
                                    negate=True).then_inc(S["s_nm"], 1)
                if b is not None:
                    if first(b):
                        weight_values()
                    if a is None:
                        dve.wait_ge(S["s_x1"], GB * b + GB)
                    for q in range(GB):
                        stat(1, b, q, S["l_stat"])
                if b is not None:
                    dve.wait_ge(S["l_stat"], GB * b + GB)
                    moments(1, b, "l_m1", "l_m2", "l_var")
                if b is not None:
                    dve.wait_ge(S["l_khi"], b + 1)
                    wait(dve, "l_kst", 64 * b)
                    V.scalar_tensor_tensor(out=klo[:, :], in0=bank(7), scalar=bcol[:, 1:2], in1=khi[:, :],
                                           op0=ALU.add, op1=ALU.subtract).then_inc(S["l_klo"], 1)
                if c is not None:
                    dve.wait_ge(S["l_qhi"], c + 1)
                    if last(c):
                        dve.wait_ge(S["s_s"], NG)
                    else:
                        wait(dve, "l_qst", 64 * c)
                    hi, lo = q_parts(c)
                    V.scalar_tensor_tensor(out=lo, in0=bank(6), scalar=bcol[:, 0:1], in1=hi,
                                           op0=ALU.add, op1=ALU.subtract).then_inc(S["l_qlo"], 1)
                if isinstance(a, int) and a == 0:
                    dve.wait_ge(S["ld_x"], 48)

            def maxima(n, s, b):
                dve.wait_ge(S["t_sn"], NSET * n + s + 1)
                if s == 0:
                    wait(dve, "t_nm", n - 1)
                V.tensor_reduce(nm[:, b % 2, JT * s:JT * s + JT], bank(s % 2).rearrange("p (j m) -> p j m", m=P),
                                AX.X, ALU.max, negate=True).then_inc(S["t_max"], 1)

            def max_high(n, b):
                dve.wait_ge(S["t_max"], NSET * n + NSET)
                wait(dve, "t_mT", n)
                V.tensor_copy(NM[:, 0:H], nm[:, b % 2, :]).then_inc(S["t_nhi"], 1)

            def max_low(n, b, residuals=0):
                dve.wait_ge(S["t_nhi"], n + 1)
                wait(dve, "t_x2", residuals)
                V.tensor_tensor(NM[:, H:2 * H], nm[:, b % 2, :], NM[:, 0:H], ALU.subtract).then_inc(S["t_nm"], 1)

            def first_maxima():
                rows2(NG - 1)
                for s in range(NSET):
                    maxima(0, s, 0)
                max_high(0, 0)
                max_low(0, 0)

            pipeline(dve, step, first_maxima)

            def attend(n):
                dve.wait_ge(S["t_tr"], n + 1)
                wait(dve, "t_o", 2 * n)
                o3 = bank(7)[:, 2 * P:4 * P].rearrange("p (h c) -> p h c", c=VW)
                V.reciprocal(orec[:, :], o3[:, :, DK]).then_inc(S["t_rec"], 1)
                dve.wait_ge(S["t_rec"], n + 1)
                wait(dve, "t_oT", n)
                for a in range(2):
                    hs = slice(a * H // 2, (a + 1) * H // 2)
                    V.tensor_tensor(on_[:, a * P // 2:(a + 1) * P // 2].rearrange("p (k j e) -> p j k e", k=2, j=JT),
                                    o3[:, hs, 0:DK].rearrange("p (j k) e -> p j k e", j=JT),
                                    bc(orec[:, hs].rearrange("p (j k) -> p j k", j=JT).unsqueeze(3),
                                       [P, JT, 2, DK]), ALU.mult).then_inc(S["t_o"], 1)

            def residual(n, g, b):
                dve.wait_ge(S["t_wo"], n + 1)
                V.tensor_tensor(seq(X, g, b), bank(7)[:, P:2 * P], seq(X, g, b), ALU.add).then_inc(S["t_x2"], 1)

            def stat3(g, b):
                V.bn_stats(norms[2]["stats"][:, 6 * (b % GB):6 * (b % GB) + 6], seq(X, g, b)).then_inc(S["u_stat"], 1)

            def moments3(g):
                dve.wait_ge(S["u_stat"], GB * g + GB)
                moments(2, g, "u_m1", "u_m2", "u_var")

            def rows3(g, bs):
                dve.wait_ge(S["u_rstd"], g + 1)
                for b in bs:
                    normalise(2, seq(X3, g, b), g, b).then_inc(S["u_x3"], 1)

            def largest3(g):
                dve.wait_ge(S["u_x3"], GB * g + GB)
                V.tensor_reduce(mxs[:, 0, bass.ds(g, 1)], grp(X3, g), AX.X, ALU.max,
                                apply_absolute_value=True).then_inc(S["u_mx"], 1)

            def cross(g):
                for b in range(GB):
                    cur = GB * g + b
                    more = not (last(g) and b == GB - 1)
                    one, two = not (first(g) and b < 1), not (first(g) and b < 2)
                    if more:
                        for s in range(3):
                            maxima(cur + 1, s, b + 1)
                    if not first(g) and b == 2:
                        rows3(g - 1, (0, 1))
                    if not first(g) and b == 3:
                        largest3(g - 1)
                    if more:
                        maxima(cur + 1, 3, b + 1)
                    if two:
                        residual(cur - 2, g, b - 2)
                    if more:
                        max_high(cur + 1, b + 1)
                        max_low(cur + 1, b + 1, cur - 1 if two else 0)
                    elif two:
                        dve.wait_ge(S["t_x2"], cur - 1)
                    if two:
                        stat3(g, b - 2)
                    if not first(g) and b == 1:
                        moments3(g - 1)
                    if not first(g) and b == 2:
                        rows3(g - 1, (2, 3))
                    if one:
                        attend(cur - 1)

            groups(dve, cross)
            residual(B - 2, NG - 1, GB - 2)
            attend(B - 1)
            residual(B - 1, NG - 1, GB - 1)

            dve.wait_ge(S["t_x2"], B)
            stat3(NG - 1, GB - 2)
            stat3(NG - 1, GB - 1)
            moments3(NG - 1)
            rows3(NG - 1, range(GB))
            largest3(NG - 1)

            n_scale, n_unit = [0], [0]

            def scales(k0, k1, unit_of):
                n_scale[0] += 1
                n, r = n_scale[0], slice(k0, k1)
                V.tensor_reduce(mx1[:, r], mxs[:, r, :], AX.X, ALU.max).then_inc(S["g_mx"], 1)
                for m in unit_of():
                    m.then_inc(S["g_unit"], 1)
                    n_unit[0] += 1
                dve.wait_ge(S["g_unit"], n_unit[0])
                dve.wait_ge(S["g_all"], n)
                V.scalar_tensor_tensor(out=sc0[:, r], in0=mxa[:, r], scalar=1.0 / AQ, in1=unit[:, r],
                                       op0=ALU.mult, op1=ALU.mult).then_inc(S["g_s0"], 1)
                dve.wait_ge(S["g_s0"], n)
                V.tensor_scalar(scale[:, r], sc0[:, r], 1e-12, None, ALU.max).then_inc(S["g_s"], 1)
                dve.wait_ge(S["g_s"], n)
                V.reciprocal(recip[:, r], scale[:, r]).then_inc(S["g_r"], 1)
                dve.wait_ge(S["g_r"], n)
                V.tensor_tensor(lev[:, r], recip[:, r], unit[:, r], ALU.mult).then_inc(S["g_lev"], 1)
                dve.wait_ge(S["g_lev"], n)

            dve.wait_ge(S["u_mx"], NG)
            scales(0, 1, lambda: [V.memset(unit[:, 0:1], 1.0)])

            def levels(g):
                if not first(g):
                    wait(dve, "a_n3", g)
                V.tensor_scalar(n3m[:, :], grp(X3, g), lev[:, 0:1], MAGIC, ALU.mult, ALU.add).then_inc(S["a_rnd"], 1)
                dve.wait_ge(S["a_rnd"], g + 1)
                if not first(g):
                    wait(dve, "a_nT", g)
                V.tensor_scalar(n3[:, :], n3m[:, :], -MAGIC, None, ALU.add).then_inc(S["a_n3"], 1)

            def largest(k, t, g, done):
                V.tensor_reduce(mxs[:, k, bass.ds(g, 1)], grp(t, g, FW), AX.X, ALU.max,
                                apply_absolute_value=True).then_inc(S[done], 1)

            def gate_largest(g):
                dve.wait_ge(S["a_gc"], FC * g + FC)
                largest(1, G, g, "a_mx")

            levels(0)
            levels(1)
            with dve.Fori(0, NG - 2) as g:
                levels(g + 2)
                gate_largest(g)
            gate_largest(NG - 2)
            gate_largest(NG - 1)
            dve.wait_ge(S["a_mx"], NG)
            scales(1, 2, lambda: [V.tensor_copy(unit[:, 1:2], scale[:, 0:1])])

            def gated_largest(g):
                dve.wait_ge(S["b_t"], g + 1)
                largest(3, GI, g, "b_mx")

            def sigmoid_turn(i):
                for u in range(2):
                    g = 2 * i + u
                    dve.wait_ge(S["b_sig"], g + 1)
                    wait(dve, "b_t", g - 1)
                    V.tensor_scalar(sq[:, u], sig[:, u], 65536.0, 65535.0, ALU.mult, ALU.min).then_inc(S["b_sq"], 1)
                    if not (isinstance(i, int) and g == 0):
                        gated_largest(g - 1)
                    if isinstance(i, int) and g == NG - 1:
                        dve.wait_ge(S["b_ng"], NG)
                        dve.wait_ge(S["b_sq"], NG)
                        V.tensor_tensor(grp(GI, NG - 1, FW), ng[:, 1], sq[:, 1], ALU.mult).then_inc(S["b_t7"], 1)
                    dve.wait_ge(S["b_uc"], FC * g + FC)
                    largest(2, U, g, "b_umx")

            pairs(dve, sigmoid_turn)
            dve.wait_ge(S["b_t7"], 1)
            largest(3, GI, NG - 1, "b_mx")
            dve.wait_ge(S["b_mx"], NG)
            dve.wait_ge(S["b_umx"], NG)
            scales(2, 4, lambda: [V.tensor_copy(unit[:, 2:3], scale[:, 0:1]),
                                  V.tensor_scalar(unit[:, 3:4], scale[:, 1:2], 1.0 / 65536.0, None, ALU.mult)])

            with dve.Fori(0, NG // 2) as i:
                dve.wait_ge(S["c_tn"], 2 * i + 1)
                dve.wait_ge(S["c_un"], 2 * i + 1)
                V.tensor_tensor(GI[:, bass.ds(i * 2 * FW + PW, FW - PW)], tn[:, 0, PW:FW], un[:, 0, PW:FW], ALU.mult
                                ).then_inc(S["c_o2"], 1)
                dve.wait_ge(S["c_tn"], 2 * i + 2)
                dve.wait_ge(S["c_un"], 2 * i + 2)
                V.tensor_tensor(grp(GI, 2 * i + 1, FW), tn[:, 1], un[:, 1], ALU.mult).then_inc(S["c_o1"], 1)
                dve.wait_ge(S["c_o0"], i + 1)
                dve.wait_ge(S["c_o2"], i + 1)
                largest(4, GI, 2 * i, "c_mx")
                dve.wait_ge(S["c_o1"], i + 1)
                largest(4, GI, 2 * i + 1, "c_mx")
            dve.wait_ge(S["c_mx"], NG)
            scales(4, 5, lambda: [V.tensor_tensor(unit[:, 4:5], scale[:, 3:4], scale[:, 2:3], ALU.mult)])

            def product_levels(g, u):
                dve.wait_ge(S["d_oq"], g + 1)
                wait(dve, "d_y", g - 1)
                V.tensor_copy(on[:, u], oq[:, u]).then_inc(S["d_on"], 1)

            def result(g, u, i):
                dve.wait_ge(S["d_y"], g + 1)
                wait(dve, "d_st%d" % u, 16 * i)
                V.scalar_tensor_tensor(out=y[:, u], in0=bank(u), scalar=scale[:, 4:5], in1=grp(X, g),
                                       op0=ALU.mult, op1=ALU.add).then_inc(S["d_yc"], 1)

            def down_turn(i):
                product_levels(2 * i, 0)
                if not (isinstance(i, int) and i == 0):
                    result(2 * i - 1, 1, i - 1)
                product_levels(2 * i + 1, 1)
                result(2 * i, 0, i)

            down_turn(0)
            down_turn(1)
            with dve.Fori(2, NG // 2) as i:
                down_turn(i)
            result(NG - 1, 1, NG // 2 - 1)


_INS = ["x", "ctx_1024", "mask_Bx1xS2_ik0", "L0_attn_W_qkv", "L0_xattn_Wq", "L0_xattn_bq", "L0_xattn_Wk",
        "L0_xattn_bk", "L0_xattn_Wv", "L0_xattn_bv", "L0_xattn_Wo", "L0_xattn_bo", "L0_ffn_w_gate",
        "L0_ffn_w_up", "L0_ffn_w_down"]
_OUTS = [((32, 128, 128), "float32")]


def kernel(**inputs):
    import numpy as _np
    import concourse.bacc as _bacc
    from concourse import mybir as _mybir
    from concourse.bass_utils import run_bass_kernel_spmd as _run

    nc = _bacc.Bacc("TRN2", target_bir_lowering=False, num_devices=1)
    arrays, args = {}, []
    for name in _INS:
        a = _np.ascontiguousarray(inputs[name])
        arrays[f"in_{name}_dram"] = a
        args.append(nc.dram_tensor(f"in_{name}_dram", a.shape, _mybir.dt.from_np(a.dtype), kind="ExternalInput").ap())
    for i, (shape, dtype) in enumerate(_OUTS):
        dt = _mybir.dt.from_np(_np.dtype(dtype))
        args.append(nc.dram_tensor(f"out_{i}_dram", shape, dt, kind="ExternalOutput").ap())
    decoder(nc, *args)
    r = _run(nc, [arrays], core_ids=[0])
    got = tuple(r.results[0][f"out_{i}_dram"] for i in range(len(_OUTS)))
    return got[0]
```
